# Optimizing a Trainium2 kernel written in Bass

```python
import numpy as np
import jax
import jax.numpy as jnp

def _softmax(x, axis=-1):
    return jax.nn.softmax(x, axis=axis)

def _gelu(x):
    return jax.nn.gelu(x, approximate=True)

def _silu(x):
    return jax.nn.silu(x)

def _sigmoid(x):
    return jax.nn.sigmoid(x)

def _layernorm(x, axis=-1, eps=1e-05):
    m = jnp.mean(x, axis=axis, keepdims=True)
    v = jnp.var(x, axis=axis, keepdims=True)
    return (x - m) / jnp.sqrt(v + eps)

def _scatter_add(tgt, idx, src, axis=0):
    return tgt.at[idx].add(src)

def _segment_sum(src, seg, n):
    return jax.ops.segment_sum(src, seg, n)
kernel_name = 'mk_xattn_ffn_d1_seqx_r8_b85a6a'

def setup_inputs(seed: int=0):
    np.random.seed(seed)
    _w = jnp.asarray

    def _rec_inputs():
        import jax
        import jax.numpy as jnp
        _rk = jax.random.key(seed)
        x = -0.000125 + 0.9999 * jax.random.normal(jax.random.fold_in(_rk, 1), (4, 256, 256), jnp.float32)
        _lenS = 256 - jax.random.randint(jax.random.fold_in(_rk, 7), (4,), 0, max(1, 256 // 4) + 1, jnp.int32)
        _lenS2 = 256 - jax.random.randint(jax.random.fold_in(_rk, 8), (4,), 0, max(1, 256 // 4) + 1, jnp.int32)
        itok_BxS_13_99985 = jax.random.randint(jax.random.fold_in(_rk, 11), (4, 256), 13, 99986, jnp.int32)
        _ctx_2048P = jax.random.normal(jax.random.fold_in(_rk, 12), (4, 16, 256), jnp.float32)
        _ctx_2048c = jax.random.dirichlet(jax.random.fold_in(_rk, 512), 0.3 * jnp.ones((16,), jnp.float32), (4, 256))
        _ctx_2048t = jnp.einsum('bsk,bkd->bsd', _ctx_2048c, _ctx_2048P)
        _ctx_2048t = _ctx_2048t * jax.lax.rsqrt(jnp.mean(jnp.square(_ctx_2048t)) + 1e-12) * 0.953939
        ctx_2048 = 6.82029e-06 + 0.0200006 * (_ctx_2048t + 0.3 * jax.random.normal(jax.random.fold_in(_rk, 612), (4, 256, 256), jnp.float32))
        return (x, itok_BxS_13_99985, ctx_2048)
    x, itok_BxS_13_99985, ctx_2048 = _rec_inputs()

    def _L0_xattn_setup():
        import jax, jax.numpy as jnp
        import numpy as np
        B, S, D = (4, 512, 256)
        E = 4
        F = 1024 // E
        VOCAB = 12500
        key = jax.random.key(seed)
        k1, k2, k3, k4, k5 = jax.random.split(key, 5)
        hidden_states = jax.random.normal(k1, (B, S, D), dtype=jnp.float32)
        token_ids = jax.random.randint(k2, (B, S), 0, VOCAB, dtype=jnp.int64)
        Wg = jax.random.normal(k3, (E, F, D), dtype=jnp.float32) * 0.02
        Wu = jax.random.normal(k4, (E, F, D), dtype=jnp.float32) * 0.02
        Wd = jax.random.normal(k5, (E, D, F), dtype=jnp.float32) * 0.02
        return {'hidden_states': hidden_states, 'token_ids': token_ids, 'Wg': Wg, 'Wu': Wu, 'Wd': Wd}
    _L0_xattn_all = _L0_xattn_setup()
    _L0_xattn_in = {k: v for k, v in _L0_xattn_all.items() if k in ()}
    del _L0_xattn_all

    def _L0_ffn_setup():
        import jax, jax.numpy as jnp
        import numpy as np
        B, S, D = (4, 512, 256)
        DFF = 4 * D
        SKIP = 0.125
        key = jax.random.key(seed)
        ks = jax.random.split(key, 4)
        s_in = 1.0 / np.sqrt(D).astype(np.float32)
        s_ff = 1.0 / np.sqrt(DFF).astype(np.float32)
        return {'x': jax.random.normal(ks[0], (B, S, D), jnp.float32), 'Wr': jax.random.normal(ks[1], (D, 1), jnp.float32) * s_in, 'br': jnp.zeros((1,), jnp.float32), 'W1': jax.random.normal(ks[2], (D, DFF), jnp.float32) * s_in, 'b1': jnp.zeros((DFF,), jnp.float32), 'W2': jax.random.normal(ks[3], (DFF, D), jnp.float32) * s_ff, 'b2': jnp.zeros((D,), jnp.float32)}
    _L0_ffn_all = _L0_ffn_setup()
    _L0_ffn_in = {k: v for k, v in _L0_ffn_all.items() if k in ('Wr', 'br', 'W1', 'b1', 'W2', 'b2')}
    del _L0_ffn_all
    return {'x': x, 'itok_BxS_13_99985': itok_BxS_13_99985, 'ctx_2048': ctx_2048, 'L0_ffn_Wr': _L0_ffn_in['Wr'], 'L0_ffn_br': _L0_ffn_in['br'], 'L0_ffn_W1': _L0_ffn_in['W1'], 'L0_ffn_b1': _L0_ffn_in['b1'], 'L0_ffn_W2': _L0_ffn_in['W2'], 'L0_ffn_b2': _L0_ffn_in['b2']}

def reference(x, itok_BxS_13_99985, ctx_2048, L0_ffn_Wr, L0_ffn_br, L0_ffn_W1, L0_ffn_b1, L0_ffn_W2, L0_ffn_b2):
    import jax
    import jax.numpy as jnp

    def _L0_xattn_ref(hidden_states, token_ids, Wg, Wu, Wd):
        import jax, jax.numpy as jnp
        import numpy as np
        B, S, D = (4, 512, 256)
        E = 4
        F = 1024 // E
        VOCAB = 12500
        tokens_per_expert = VOCAB // E
        tid = jnp.clip(token_ids, 0, VOCAB - 1)
        expert_ids = jnp.minimum(tid // tokens_per_expert, E - 1)
        out = jnp.zeros_like(hidden_states)
        for e in range(E):
            g = jax.nn.silu(jnp.einsum('bsd,fd->bsf', hidden_states, Wg[e]))
            u = jnp.einsum('bsd,fd->bsf', hidden_states, Wu[e])
            y = jnp.einsum('bsf,df->bsd', g * u, Wd[e])
            out = jnp.where((expert_ids == e)[..., None], y, out)
        return out

    def _L0_ffn_ref(x, Wr, br, W1, b1, W2, b2):
        import jax, jax.numpy as jnp
        import numpy as np
        B, S, D = (4, 512, 256)
        DFF = 4 * D
        SKIP = 0.125
        Bs, Ss, Ds = x.shape
        k = max(int(Ss * SKIP), 1)
        logits = (x @ Wr + br)[..., 0]
        weights, idx = jax.lax.top_k(logits, k)
        perm = jnp.argsort(idx, axis=1)
        tokens = jnp.take_along_axis(idx, perm, axis=1)
        fx = jnp.take_along_axis(x, tokens[..., None], axis=1)
        h = jax.nn.gelu(fx @ W1 + b1, approximate=False)
        out_l = h @ W2 + b2
        tw = jax.nn.softmax(weights, axis=1)
        rw = jnp.take_along_axis(tw, perm, axis=1)
        xw = rw[..., None] * out_l
        bidx = jnp.arange(Bs)[:, None]
        return x.at[bidx, tokens].add(xw)
    x = x + _L0_xattn_ref(_layernorm(x, axis=-1), itok_BxS_13_99985, ctx_2048, ctx_2048, ctx_2048)
    x = x + _L0_ffn_ref(_layernorm(x, axis=-1), L0_ffn_Wr, L0_ffn_br, L0_ffn_W1, L0_ffn_b1, L0_ffn_W2, L0_ffn_b2)
    return x

_drawn_inputs = setup_inputs


def setup_inputs(seed=0):
    import zlib

    import numpy as np

    out = dict(_drawn_inputs(seed))
    spreads = {'L0_ffn_b1': (0.0, 0.8), 'L0_ffn_b2': (0.0, 2.0)}
    factors = {'L0_ffn_Wr': 7.189, 'L0_ffn_W1': 5.754, 'L0_ffn_W2': 5.368}
    for name, (base, spread) in spreads.items():
        noise = np.random.default_rng([zlib.crc32(name.encode()), seed]).standard_normal(out[name].shape)
        drawn = base * np.exp(spread * noise) if base else spread * noise
        out[name] = jnp.asarray(drawn.astype(out[name].dtype))
    for name, factor in factors.items():
        out[name] = (out[name] * factor).astype(out[name].dtype)
    return out
```

```python
from contextlib import ExitStack

import concourse.bass as bass
from concourse import mybir

F32 = mybir.dt.float32
F32R = mybir.dt.float32r
I32 = mybir.dt.int32
ALU = mybir.AluOpType
ACT = mybir.ActivationFunctionType
AX_X = mybir.AxisListType.X

P = 128
VOCAB = 12500
EPS = 1e-5
NOT_CHOSEN = 1000.0


def fused_layers(nc, x, tokens, wT, wr, br, w1, b1, w2, b2, out):
    B, S, D = x.shape
    E = wT.shape[0]
    DFF = w1.shape[1]
    NK = D // P
    NJ = S // P
    NT = B * NJ
    NF = DFF // P
    TOP = S // 8
    SLOTS = B * TOP
    PER_EXPERT = VOCAB // E
    assert (NK, NJ, SLOTS) == (2, 2, P)

    x_tiles = x.rearrange("b (j p) d -> p (b j) d", p=P)
    out_tiles = out.rearrange("b (j p) d -> p (b j) d", p=P)
    wT_tiles = wT.rearrange("e (k p) r -> e p k r", p=P)
    w1_tiles = w1.rearrange("(k p) f -> p k f", p=P)
    w2_tiles = w2.rearrange("(f p) d -> p f d", p=P)

    with ExitStack() as ctx:
        def sb(name, shape, dt=F32):
            return ctx.enter_context(nc.sbuf_tensor(name, shape, dt))

        def psum(name, shape):
            return ctx.enter_context(nc.psum_tensor(name, shape, F32))

        def sem(name):
            return ctx.enter_context(nc.semaphore(name))

        x_in = sb("x_in", [P, NT, D])
        tok = sb("tok", [P, NT], I32)
        wT_in = sb("wT_in", [P, E, NK, D])
        w1_in = sb("w1_in", [P, NK, DFF])
        w2_in = sb("w2_in", [P, NF, D])
        wr_all = sb("wr_all", [P, D])
        br_all = sb("br_all", [P, 1])
        b1_cols = sb("b1_cols", [P, NF])
        b2_row = sb("b2_row", [1, D])
        col_minus_row = sb("col_minus_row", [P, S], I32)
        slot_of_batch = sb("slot_of_batch", [P, B, SLOTS], I32)
        ident = sb("ident", [P, P])
        earlier = sb("earlier", [P, NJ, S])
        ones = sb("ones", [P, P])
        minus_half = sb("minus_half", [P, NJ])
        at_least = sb("at_least", [P, E + 1, NT])
        mask = sb("mask", [P, E, NT])
        w_hi = sb("w_hi", [P, E, NK, D], F32R)
        w_lo = sb("w_lo", [P, E, NK, D], F32R)
        stats = sb("stats", [P, NJ, 6])
        mean_var = sb("mean_var", [P, NJ, 2])
        var_eps = sb("var_eps", [P, NJ])
        rstd = sb("rstd", [P, NJ])
        xn = sb("xn", [P, NJ, D])
        xT_hi = sb("xT_hi", [P, B, NK, S], F32R)
        xT_lo = sb("xT_lo", [P, B, NK, S], F32R)
        silu = sb("silu", [P, 2, NK, S])
        gu = sb("gu", [P, 2, NK, S])
        gu_hi = sb("gu_hi", [P, 2, NK, S], F32R)
        gu_lo = sb("gu_lo", [P, 2, NK, S], F32R)
        x1 = sb("x1", [P, NT, D])
        stats2 = sb("stats2", [P, NJ, 6])
        mean_var2 = sb("mean_var2", [P, NJ, 2])
        var_eps2 = sb("var_eps2", [P, NJ])
        rstd2 = sb("rstd2", [P, NJ])
        xn2 = sb("xn2", [P, NJ, D])
        base = sb("base", [P, NT, D])
        product = sb("product", [P, NJ, D])
        logits = sb("logits", [P, NT])
        diag = sb("diag", [P, NJ, P])
        above = sb("above", [P, NJ])
        tied = sb("tied", [P, NJ])
        scratch_above = sb("scratch_above", [P, NJ, S])
        scratch_tied = sb("scratch_tied", [P, NJ, S])
        rank = sb("rank", [P, NT])
        slot_rank = sb("slot_rank", [P, NJ])
        select = sb("select", [P, NJ, SLOTS])
        selectT = sb("selectT", [P, NT, P], F32R)
        top_logit = sb("top_logit", [P, B])
        shifted = sb("shifted", [P, NT])
        expo = sb("expo", [P, NT])
        expo_top = sb("expo_top", [P, NT])
        expo_sum = sb("expo_sum", [P, B])
        expo_inv = sb("expo_inv", [P, B])
        weight = sb("weight", [P, NT])
        fxT = sb("fxT", [P, NK, SLOTS])
        gT = sb("gT", [P, NF, SLOTS])
        ffn = sb("ffn", [P, D])
        ffn_hi = sb("ffn_hi", [P, D], F32R)
        ffn_lo = sb("ffn_lo", [P, D], F32R)
        result = sb("result", [P, NT, D])

        h_ps = [psum(f"h_ps{i}", [P, NK, S]) for i in range(2)]
        y_ps = [psum(f"y_ps{i}", [P, NJ, D]) for i in range(2)]
        xT_ps = psum("xT_ps", [P, NK, S])
        logit_ps = psum("logit_ps", [P, S])
        fxT_ps = psum("fxT_ps", [P, 2 * NK, SLOTS])
        selT_ps = psum("selT_ps", [P, 4, P])
        ffn_ps = logit_ps
        sum_ps = xT_ps[:, 0, 0:NT]

        d_x = [sem(f"d_x{b}") for b in range(B)]
        d_tok = sem("d_tok")
        d_wT = [sem(f"d_wT{e}") for e in range(E)]
        d_wr = sem("d_wr")
        d_b = sem("d_b")
        d_w1 = sem("d_w1")
        d_w2 = sem("d_w2")
        d_out = sem("d_out")
        s_iota = sem("s_iota")
        s_const = sem("s_const")
        s_half = sem("s_half")
        s_geq = sem("s_geq")
        s_mask = sem("s_mask")
        s_whi = sem("s_whi")
        s_wlo = sem("s_wlo")
        s_stats = sem("s_stats")
        s_mean = sem("s_mean")
        s_veps = sem("s_veps")
        s_rstd = sem("s_rstd")
        s_xn = sem("s_xn")
        s_xTps = sem("s_xTps")
        s_xhi = sem("s_xhi")
        s_xlo = sem("s_xlo")
        s_h = sem("s_h")
        s_silu = sem("s_silu")
        s_gu = sem("s_gu")
        s_ghi = sem("s_ghi")
        s_glo = sem("s_glo")
        s_y = sem("s_y")
        s_x1 = sem("s_x1")
        s_stats2 = sem("s_stats2")
        s_mean2 = sem("s_mean2")
        s_veps2 = sem("s_veps2")
        s_rstd2 = sem("s_rstd2")
        s_xn2 = sem("s_xn2")
        s_base = sem("s_base")
        s_logit = sem("s_logit")
        s_diag = sem("s_diag")
        s_lrow = sem("s_lrow")
        s_count = sem("s_count")
        s_rank = sem("s_rank")
        s_top = sem("s_top")
        s_srank = sem("s_srank")
        s_select = sem("s_select")
        s_selT = sem("s_selT")
        s_selTsb = sem("s_selTsb")
        s_gather = sem("s_gather")
        s_fx = sem("s_fx")
        s_shift = sem("s_shift")
        s_exp = sem("s_exp")
        s_etop = sem("s_etop")
        s_sum = sem("s_sum")
        s_esum = sem("s_esum")
        s_einv = sem("s_einv")
        s_weight = sem("s_weight")
        s_hid = sem("s_hid")
        s_g = sem("s_g")
        s_ffn = sem("s_ffn")
        s_fhi = sem("s_fhi")
        s_flo = sem("s_flo")
        s_add = sem("s_add")
        s_res = sem("s_res")

        def wait(eng, semaphore, value):
            if not isinstance(value, int) or value > 0:
                eng.wait_ge(semaphore, value)

        block = ctx.enter_context(nc.Block())

        @block.sync
        def _(sp):
            sp.dma_start(x_in[:, 0:NJ, :], x_tiles[:, 0:NJ, :]).then_inc(d_x[0], 16)
            sp.dma_start(wT_in[:, 1], wT_tiles[1]).then_inc(d_wT[1], 16)
            sp.dma_start(tok[:, :], tokens).then_inc(d_tok, 16)
            sp.dma_start(x_in[:, NJ:2 * NJ, :], x_tiles[:, NJ:2 * NJ, :]).then_inc(d_x[1], 16)
            sp.dma_start(wT_in[:, 3], wT_tiles[3]).then_inc(d_wT[3], 16)
            sp.dma_start(br_all[:, :], br.partition_broadcast(P)).then_inc(d_wr, 16)
            sp.dma_start(wr_all[:, :], wr.partition_broadcast(P)).then_inc(d_wr, 16)
            for b in range(2, B):
                sp.dma_start(x_in[:, NJ * b:NJ * b + NJ, :], x_tiles[:, NJ * b:NJ * b + NJ, :]).then_inc(d_x[b], 16)
            sp.dma_start(b1_cols[:, :], b1).then_inc(d_b, 16)
            sp.dma_start(b2_row[:, :], b2).then_inc(d_b, 16)
            sp.dma_start(w1_in[:, :, :], w1_tiles).then_inc(d_w1, 16)
            sp.dma_start(w2_in[:, :, :], w2_tiles).then_inc(d_w2, 16)
            for b in range(B):
                sp.wait_ge(s_res, NJ * b + NJ)
                sp.dma_start(out_tiles[:, NJ * b:NJ * b + NJ, :], result[:, NJ * b:NJ * b + NJ, :]).then_inc(d_out, 16)
            sp.wait_ge(d_out, 16 * B)

        @block.tensor
        def _(pe):
            def transpose_xn(b):
                pe.wait_ge(s_xn, b + 1)
                wait(pe, s_xlo, b)
                for k in range(NK):
                    for j in range(NJ):
                        mm = pe.transpose(xT_ps[:, k, P * j:P * j + P], xn[:, j, P * k:P * k + P], ident[:, :])
                mm.then_inc(s_xTps, 1)

            def layer1(b, e):
                u = E * b + e
                pe.wait_ge(s_xlo, b + 1)
                if isinstance(b, int) and b == 0:
                    pe.wait_ge(s_wlo, e + 1)
                wait(pe, s_gu, u - 1)
                for f in range(NK):
                    rows = slice(P * f, P * f + P)
                    n = 0
                    for k in range(NK):
                        for w, v in ((w_hi, xT_hi), (w_hi, xT_lo), (w_lo, xT_hi)):
                            mm = pe.matmul(h_ps[e % 2][:, f, :], w[:, e, k, rows], v[:, b, k, :],
                                           start=(n == 0), stop=(n == 3 * NK - 1))
                            n += 1
                mm.then_inc(s_h, 1)

            def layer2(b, e):
                u = E * b + e
                pe.wait_ge(s_glo, u + 1)
                wait(pe, s_x1, NJ * (u - 1))
                for j in range(NJ):
                    cols = slice(P * j, P * j + P)
                    n = 0
                    for k in range(NK):
                        for g, w in ((gu_hi, w_hi), (gu_hi, w_lo), (gu_lo, w_hi)):
                            mm = pe.matmul(y_ps[e % 2][:, j, :], g[:, e % 2, k, cols], w[:, e, k, :],
                                           start=(n == 0), stop=(n == 3 * NK - 1))
                            n += 1
                mm.then_inc(s_y, 1)

            def logit_row(b):
                pe.wait_ge(s_diag, b + 1)
                wait(pe, s_top, b)
                for j in range(NJ):
                    mm = pe.matmul(logit_ps[:, P * j:P * j + P], ones[:, :], diag[:, j, :], start=True, stop=True)
                mm.then_inc(s_lrow, 1)

            def gather(b):
                pe.wait_ge(s_select, b + 1)
                wait(pe, s_selTsb, b)
                for j in range(NJ):
                    mm = pe.transpose(selT_ps[:, j, :], select[:, j, :], ident[:, :])
                mm.then_inc(s_selT, 1)
                for k in range(NK):
                    for j in range(NJ):
                        first = isinstance(b, int) and b == 0 and (k, j) == (0, 0)
                        mm = pe.matmul(fxT_ps[:, k, :], xn2[:, j, P * k:P * k + P], select[:, j, :],
                                       start=first, stop=False, skip_group_check=True)
                mm.then_inc(s_gather, 1)

            def batch(b, first=False, last=False):
                layer1(b, 1)
                layer2(b, 0)
                layer1(b, 2)
                layer2(b, 1)
                if not last:
                    transpose_xn(b + 1)
                layer1(b, 3)
                if not first:
                    logit_row(b - 1)
                layer2(b, 2)
                if not last:
                    layer1(b + 1, 0)
                layer2(b, 3)
                if not first:
                    gather(b - 1)

            pe.wait_ge(s_const, 1)
            transpose_xn(0)
            layer1(0, 0)
            pe.wait_ge(s_const, 3)
            batch(0, first=True)
            for b in range(1, B - 1):
                batch(b)
            batch(B - 1, last=True)
            logit_row(B - 1)
            gather(B - 1)

            hid = [t[:, i, :] for t in (h_ps[0], h_ps[1], y_ps[0], y_ps[1]) for i in range(1)]
            pe.wait_ge(s_fx, 1)
            pe.wait_ge(d_w1, 16)
            pe.wait_ge(d_w2, 16)
            pe.wait_ge(d_b, 32)
            pe.wait_ge(s_top, B)
            pe.matmul(ffn_ps[:, :], ones[0:1, :], b2_row[:, :], start=True, stop=False)

            def ffn_out(f):
                pe.wait_ge(s_g, f + 1)
                return pe.matmul(ffn_ps[:, :], gT[:, f, :], w2_in[:, f, :], start=False, stop=(f == NF - 1))

            for f in range(NF):
                wait(pe, s_g, f - 3)
                for k in range(NK):
                    mm = pe.matmul(hid[f % 4][:, 0:SLOTS], w1_in[:, k, P * f:P * f + P], fxT[:, k, :],
                                   start=(k == 0), stop=(k == NK - 1))
                mm.then_inc(s_hid, 1)
                if f >= 2:
                    ffn_out(f - 2)
            ffn_out(NF - 2)
            ffn_out(NF - 1).then_inc(s_ffn, 1)
            pe.wait_ge(s_etop, 1)
            pe.matmul(sum_ps, ones[:, :], expo_top[:, :], start=True, stop=True).then_inc(s_sum, 1)

            pe.wait_ge(s_selTsb, B)
            pe.wait_ge(s_fhi, 1)
            for t in range(NT):
                bank = (h_ps[0], h_ps[1], y_ps[0], y_ps[1])[t // 2]
                pe.matmul(bank[:, t % 2, :], selectT[:, t, :], ffn_hi[:, :], start=True, stop=False)
                pe.wait_ge(s_flo, 1)
                mm = pe.matmul(bank[:, t % 2, :], selectT[:, t, :], ffn_lo[:, :], start=False, stop=True)
                if t % 2:
                    mm.then_inc(s_add, 1)

        @block.scalar
        def _(act):
            act.dma_start(wT_in[:, 0], wT_tiles[0]).then_inc(d_wT[0], 16)
            act.dma_start(wT_in[:, 2], wT_tiles[2]).then_inc(d_wT[2], 16)
            act.preload_act_table(ACT.Silu)

            def split_w(e):
                act.wait_ge(d_wT[e], 16)
                act.activation(w_hi[:, e], wT_in[:, e], ACT.Copy).then_inc(s_whi, 1)

            def split_x(b):
                act.wait_ge(s_xTps, b + 1)
                act.activation(xT_hi[:, b], xT_ps[:, :, :], ACT.Copy).then_inc(s_xhi, 1)

            def unit(b, e):
                u = E * b + e
                act.wait_ge(s_h, u + 1)
                wait(act, s_gu, u - 1)
                act.activation(silu[:, e % 2], h_ps[e % 2][:, :, :], ACT.Silu).then_inc(s_silu, 1)
                act.wait_ge(s_gu, u + 1)
                wait(act, s_y, u - 1)
                act.activation(gu_hi[:, e % 2], gu[:, e % 2], ACT.Copy).then_inc(s_ghi, 1)

            def diagonal(b):
                act.wait_ge(s_logit, b + 1)
                wait(act, s_lrow, b)
                for j in range(NJ):
                    t = NJ * b + j
                    d = act.activation(diag[:, j, :], ident[:, :], ACT.Copy, scale=logits[:, t:t + 1])
                d.then_inc(s_diag, 1)

            def keep_selectT(b):
                act.wait_ge(s_selT, b + 1)
                act.activation(selectT[:, NJ * b:NJ * b + NJ, :], selT_ps[:, 0:NJ, :], ACT.Copy).then_inc(s_selTsb, 1)

            def batch(b, first=False, last=False):
                unit(b, 1)
                unit(b, 2)
                if not first:
                    diagonal(b - 1)
                if not last:
                    split_x(b + 1)
                unit(b, 3)
                if not last:
                    unit(b + 1, 0)
                if not first:
                    keep_selectT(b - 1)

            split_w(0)
            split_x(0)
            split_w(1)
            unit(0, 0)
            split_w(2)
            split_w(3)
            act.wait_ge(s_const, 1)
            batch(0, first=True)
            for b in range(1, B - 1):
                batch(b)
            batch(B - 1, last=True)
            act.preload_act_table(ACT.Exp)
            diagonal(B - 1)
            act.wait_ge(s_shift, 1)
            act.activation(expo[:, :], shifted[:, :], ACT.Exp).then_inc(s_exp, 1)
            act.preload_act_table(ACT.Gelu)
            keep_selectT(B - 1)
            hid = [t[:, 0, :] for t in (h_ps[0], h_ps[1], y_ps[0], y_ps[1])]
            act.wait_ge(d_b, 32)
            for f in range(NF):
                act.wait_ge(s_hid, f + 1)
                act.activation(gT[:, f, :], hid[f % 4][:, 0:SLOTS], ACT.Gelu, bias=b1_cols[:, f:f + 1]).then_inc(s_g, 1)
            act.wait_ge(s_ffn, 1)
            act.activation(ffn_hi[:, :], ffn_ps[:, :], ACT.Copy).then_inc(s_fhi, 1)

        @block.gpsimd
        def _(pool):
            pool.iota(col_minus_row[:, :], [[1, S]], base=0, channel_multiplier=-1).then_inc(s_iota, 1)
            pool.memset(minus_half[:, :], -0.5).then_inc(s_half, 1)

            def inverse_root(b, mean, source, shifted_var, target, signal_shift, signal):
                pool.wait_ge(mean, b + 1)
                pool.tensor_scalar(shifted_var[:, :], source[:, :, 1], EPS, None, ALU.add).then_inc(signal_shift, 1)
                pool.wait_ge(signal_shift, b + 1)
                pool.tensor_tensor(target[:, :], shifted_var[:, :], minus_half[:, :], ALU.pow).then_inc(signal, 1)

            def rstd_x(b):
                inverse_root(b, s_mean, mean_var, var_eps, rstd, s_veps, s_rstd)

            def rstd_x1(b):
                inverse_root(b, s_mean2, mean_var2, var_eps2, rstd2, s_veps2, s_rstd2)

            def split_w(e):
                pool.wait_ge(s_whi, e + 1)
                pool.tensor_tensor(w_lo[:, e], wT_in[:, e], w_hi[:, e].bitcast(F32), ALU.subtract).then_inc(s_wlo, 1)

            def low_part(b, e):
                u = E * b + e
                pool.wait_ge(s_ghi, u + 1)
                wait(pool, s_y, u - 1)
                pool.tensor_tensor(gu_lo[:, e % 2], gu[:, e % 2], gu_hi[:, e % 2].bitcast(F32),
                                   ALU.subtract).then_inc(s_glo, 1)

            def add_base(b):
                pool.wait_ge(s_xn2, b + 1)
                pool.tensor_tensor(base[:, NJ * b:NJ * b + NJ, :], x1[:, NJ * b:NJ * b + NJ, :], xn2[:, :, :],
                                   ALU.add).then_inc(s_base, 1)

            def batch(b, first=False, last=False):
                if not first:
                    rstd_x1(b - 1)
                if not last:
                    rstd_x(b + 1)
                low_part(b, 1)
                low_part(b, 2)
                if not first:
                    add_base(b - 1)
                low_part(b, 3)
                if not last:
                    low_part(b + 1, 0)

            pool.wait_ge(s_half, 1)
            rstd_x(0)
            split_w(0)
            pool.iota(slot_of_batch[:, :, :], [[-TOP, B], [1, SLOTS]], base=0, channel_multiplier=0).then_inc(s_iota, 1)
            split_w(1)
            low_part(0, 0)
            split_w(2)
            split_w(3)
            batch(0, first=True)
            for b in range(1, B - 1):
                batch(b)
            batch(B - 1, last=True)
            rstd_x1(B - 1)
            add_base(B - 1)

        @block.vector
        def _(dve):
            def statistics(b, source, st, mv, signal_st, signal):
                for j in range(NJ):
                    dve.bn_stats(st[:, j, :], source[:, NJ * b + j, :]).then_inc(signal_st, 1)
                dve.wait_ge(signal_st, NJ * b + NJ)
                for j in range(NJ):
                    aggr = dve.bn_aggr(mv[:, j, :], st[:, j, :])
                aggr.then_inc(signal, 1)

            def stats_x(b):
                if isinstance(b, int):
                    dve.wait_ge(d_x[b], 16)
                wait(dve, s_mean, b)
                wait(dve, s_xn, b)
                wait(dve, s_veps, b)
                statistics(b, x_in, stats, mean_var, s_stats, s_mean)

            def stats_x1(b):
                wait(dve, s_mean2, b)
                wait(dve, s_xn2, b)
                wait(dve, s_veps2, b)
                dve.wait_ge(s_x1, NJ * E * (b + 1))
                statistics(b, x1, stats2, mean_var2, s_stats2, s_mean2)

            def normalise_x(b):
                dve.wait_ge(s_rstd, b + 1)
                wait(dve, s_xTps, b)
                for j in range(NJ):
                    n = dve.tensor_scalar(xn[:, j, :], x_in[:, NJ * b + j, :], mean_var[:, j, 0:1], rstd[:, j:j + 1],
                                          ALU.subtract, ALU.mult)
                n.then_inc(s_xn, 1)

            def normalise_x1(b):
                dve.wait_ge(s_rstd2, b + 1)
                wait(dve, s_gather, b)
                wait(dve, s_base, b)
                for j in range(NJ):
                    n = dve.tensor_scalar(xn2[:, j, :], x1[:, NJ * b + j, :], mean_var2[:, j, 0:1], rstd2[:, j:j + 1],
                                          ALU.subtract, ALU.mult)
                n.then_inc(s_xn2, 1)

            def router(b):
                dve.wait_ge(s_xn2, b + 1)
                wait(dve, s_logit, b)
                for j in range(NJ):
                    t = NJ * b + j
                    r = dve.tensor_tensor_reduce(product[:, j, :], xn2[:, j, :], wr_all[:, :], 1.0, br_all[:, 0:1],
                                                 ALU.mult, ALU.add, logits[:, t:t + 1])
                r.then_inc(s_logit, 1)

            def split_x(b):
                dve.wait_ge(s_xhi, b + 1)
                dve.tensor_tensor(xT_lo[:, b], xT_ps[:, :, :], xT_hi[:, b].bitcast(F32), ALU.subtract).then_inc(s_xlo, 1)

            def gate(b, e):
                u = E * b + e
                dve.wait_ge(s_silu, u + 1)
                wait(dve, s_glo, u - 1)
                dve.tensor_tensor(gu[:, e % 2], silu[:, e % 2], h_ps[e % 2][:, :, :], ALU.mult).then_inc(s_gu, 1)

            def accumulate(b, e):
                u = E * b + e
                dve.wait_ge(s_y, u + 1)
                for j in range(NJ):
                    t = NJ * b + j
                    if e > 0:
                        dve.wait_ge(s_x1, NJ * (u - 1) + j + 1)
                    dve.scalar_tensor_tensor(out=x1[:, t, :], in0=y_ps[e % 2][:, j, :], scalar=mask[:, e, t:t + 1],
                                             in1=(x_in if e == 0 else x1)[:, t, :], op0=ALU.mult,
                                             op1=ALU.add).then_inc(s_x1, 1)

            def ranks(b):
                dve.wait_ge(s_lrow, b + 1)
                wait(dve, s_rank, b)
                for j in range(NJ):
                    t = NJ * b + j
                    dve.tensor_scalar(scratch_above[:, j, :], logit_ps[:, :], logits[:, t:t + 1], 0.0, ALU.is_gt,
                                      ALU.add, accum_out=above[:, j:j + 1]).then_inc(s_count, 1)
                    dve.scalar_tensor_tensor(out=scratch_tied[:, j, :], in0=logit_ps[:, :], scalar=logits[:, t:t + 1],
                                             in1=earlier[:, j, :], op0=ALU.is_equal, op1=ALU.mult,
                                             accum_out=tied[:, j:j + 1]).then_inc(s_count, 1)
                dve.reduce_max(top_logit[:, b:b + 1], logit_ps[:, :], AX_X).then_inc(s_top, 1)
                dve.wait_ge(s_count, 2 * NJ * (b + 1))
                dve.tensor_tensor(rank[:, NJ * b:NJ * b + NJ], above[:, :], tied[:, :], ALU.add).then_inc(s_rank, 1)

            def choose(b):
                dve.wait_ge(s_rank, b + 1)
                wait(dve, s_gather, b)
                wait(dve, s_select, b)
                for j in range(NJ):
                    t = NJ * b + j
                    dve.tensor_scalar(slot_rank[:, j:j + 1], rank[:, t:t + 1], float(TOP), NOT_CHOSEN, ALU.is_ge,
                                      ALU.mult).then_inc(s_srank, 1)
                dve.wait_ge(s_srank, NJ * (b + 1))
                for j in range(NJ):
                    t = NJ * b + j
                    s = dve.tensor_scalar(select[:, j, :], slot_of_batch[:, b, :], slot_rank[:, j:j + 1],
                                          rank[:, t:t + 1], ALU.subtract, ALU.is_equal)
                s.then_inc(s_select, 1)

            def batch(b, first=False, last=False):
                if not first:
                    stats_x1(b - 1)
                if not last:
                    stats_x(b + 1)
                gate(b, 1)
                accumulate(b, 0)
                if not last:
                    normalise_x(b + 1)
                gate(b, 2)
                if not first:
                    normalise_x1(b - 1)
                    router(b - 1)
                accumulate(b, 1)
                if not last:
                    split_x(b + 1)
                gate(b, 3)
                accumulate(b, 2)
                if not last:
                    gate(b + 1, 0)
                if not first:
                    ranks(b - 1)
                    choose(b - 1)
                accumulate(b, 3)

            stats_x(0)
            dve.wait_ge(s_iota, 1)
            dve.tensor_scalar(ident[:, :], col_minus_row[:, 0:P], 0.0, None, ALU.is_equal).then_inc(s_const, 1)
            normalise_x(0)
            dve.wait_ge(d_tok, 16)
            dve.memset(at_least[:, 0, :], 1.0).then_inc(s_geq, 1)
            dve.memset(at_least[:, E, :], 0.0).then_inc(s_geq, 1)
            for e in range(1, E):
                dve.tensor_scalar(at_least[:, e, :], tok[:, :], float(e * PER_EXPERT), None,
                                  ALU.is_ge).then_inc(s_geq, 1)
            dve.wait_ge(s_geq, E + 1)
            dve.tensor_tensor(mask[:, :, :], at_least[:, 0:E, :], at_least[:, 1:E + 1, :],
                              ALU.subtract).then_inc(s_mask, 1)
            split_x(0)
            dve.memset(ones[:, :], 1.0).then_inc(s_const, 1)
            dve.tensor_scalar(earlier[:, 0, :], col_minus_row[:, :], 0.0, None, ALU.is_lt).then_inc(s_const, 1)
            dve.tensor_scalar(earlier[:, 1, :], col_minus_row[:, :], float(P), None, ALU.is_lt).then_inc(s_const, 1)
            gate(0, 0)
            dve.wait_ge(s_mask, 1)
            batch(0, first=True)
            dve.wait_ge(d_wr, 32)
            dve.wait_ge(s_iota, 2)
            dve.wait_ge(s_const, 4)
            for b in range(1, B - 1):
                batch(b)
            batch(B - 1, last=True)
            stats_x1(B - 1)
            normalise_x1(B - 1)
            router(B - 1)
            ranks(B - 1)
            choose(B - 1)
            dve.wait_ge(s_top, B)
            for b in range(B):
                v = dve.tensor_scalar(shifted[:, NJ * b:NJ * b + NJ], logits[:, NJ * b:NJ * b + NJ],
                                      top_logit[:, b:b + 1], None, ALU.subtract)
            v.then_inc(s_shift, 1)
            dve.wait_ge(s_gather, B)
            dve.tensor_copy(fxT[:, :, :], fxT_ps[:, 0:NK, :]).then_inc(s_fx, 1)
            dve.wait_ge(s_exp, 1)
            dve.scalar_tensor_tensor(out=expo_top[:, :], in0=rank[:, :], scalar=float(TOP), in1=expo[:, :],
                                     op0=ALU.is_lt, op1=ALU.mult).then_inc(s_etop, 1)
            dve.wait_ge(s_ffn, 1)
            dve.wait_ge(s_fhi, 1)
            dve.tensor_tensor(ffn_lo[:, :], ffn_ps[:, :], ffn_hi[:, :].bitcast(F32), ALU.subtract).then_inc(s_flo, 1)
            dve.wait_ge(s_sum, 1)
            dve.reduce_sum(expo_sum[:, :], sum_ps.rearrange("p (b j) -> p b j", j=NJ), AX_X).then_inc(s_esum, 1)
            dve.wait_ge(s_esum, 1)
            dve.reciprocal(expo_inv[:, :], expo_sum[:, :]).then_inc(s_einv, 1)
            dve.wait_ge(s_einv, 1)
            for b in range(B):
                v = dve.tensor_scalar(weight[:, NJ * b:NJ * b + NJ], expo_top[:, NJ * b:NJ * b + NJ],
                                      expo_inv[:, b:b + 1], None, ALU.mult)
            v.then_inc(s_weight, 1)
            dve.wait_ge(s_weight, 1)
            dve.wait_ge(s_base, B)
            for t in range(NT):
                bank = (h_ps[0], h_ps[1], y_ps[0], y_ps[1])[t // 2]
                dve.wait_ge(s_add, t // 2 + 1)
                dve.scalar_tensor_tensor(out=result[:, t, :], in0=bank[:, t % 2, :], scalar=weight[:, t:t + 1],
                                         in1=base[:, t, :], op0=ALU.mult, op1=ALU.add).then_inc(s_res, 1)


def kernel(x, itok_BxS_13_99985, ctx_2048, L0_ffn_Wr, L0_ffn_br, L0_ffn_W1, L0_ffn_b1, L0_ffn_W2, L0_ffn_b2):
    import numpy as np
    import concourse.bacc as bacc
    from concourse.bass_utils import run_bass_kernel_spmd

    B, S, D = x.shape
    flat = np.ascontiguousarray
    arrays = {
        "x": flat(x),
        "tokens": flat(np.asarray(itok_BxS_13_99985).reshape(-1, P).T),
        "wT": flat(np.asarray(ctx_2048).transpose(0, 2, 1)),
        "wr": flat(np.asarray(L0_ffn_Wr).reshape(D)),
        "br": flat(L0_ffn_br),
        "w1": flat(L0_ffn_W1),
        "b1": flat(np.asarray(L0_ffn_b1).reshape(-1, P).T),
        "w2": flat(L0_ffn_W2),
        "b2": flat(np.asarray(L0_ffn_b2).reshape(1, D)),
    }
    nc = bacc.Bacc("TRN2", target_bir_lowering=False, num_devices=1)
    args = [nc.dram_tensor(f"in_{n}", a.shape, mybir.dt.from_np(a.dtype), kind="ExternalInput").ap()
            for n, a in arrays.items()]
    args.append(nc.dram_tensor("out", (B, S, D), F32, kind="ExternalOutput").ap())
    fused_layers(nc, *args)
    r = run_bass_kernel_spmd(nc, [{f"in_{n}": a for n, a in arrays.items()}], core_ids=[0])
    return r.results[0]["out"]
```

```python
from contextlib import ExitStack

import concourse.bass as bass
from concourse import mybir

F32 = mybir.dt.float32
F32R = mybir.dt.float32r
I32 = mybir.dt.int32
ALU = mybir.AluOpType
ACT = mybir.ActivationFunctionType
AX_X = mybir.AxisListType.X

P = 128
VOCAB = 12500
EPS = 1e-5
NOT_CHOSEN = 1000.0
WARM_START = 12
WARM_LAYER1 = 3


def fused_layers(nc, x, tokens, wT, wr, br, w1, b1, w2, b2, out):
    B, S, D = x.shape
    E = wT.shape[0]
    DFF = w1.shape[1]
    NK = D // P
    NJ = S // P
    NT = B * NJ
    NF = DFF // P
    TOP = S // 8
    SLOTS = B * TOP
    PER_EXPERT = VOCAB // E
    assert (NK, NJ, SLOTS) == (2, 2, P)

    x_tiles = x.rearrange("b (j p) d -> p (b j) d", p=P)
    out_tiles = out.rearrange("b (j p) d -> p (b j) d", p=P)
    wT_tiles = wT.rearrange("e (k p) r -> e p k r", p=P)
    w1_tiles = w1.rearrange("(k p) f -> p k f", p=P)
    w2_tiles = w2.rearrange("(f p) d -> p f d", p=P)

    with ExitStack() as ctx:
        def sb(name, shape, dt=F32):
            return ctx.enter_context(nc.sbuf_tensor(name, shape, dt))

        def psum(name, shape):
            return ctx.enter_context(nc.psum_tensor(name, shape, F32))

        def sem(name):
            return ctx.enter_context(nc.semaphore(name))

        x_in = sb("x_in", [P, NT, D])
        tok = sb("tok", [P, NT], I32)
        wT_in = sb("wT_in", [P, E, NK, D])
        w1_in = sb("w1_in", [P, NK, DFF])
        w2_in = sb("w2_in", [P, NF, D])
        wr_all = sb("wr_all", [P, D])
        br_all = sb("br_all", [P, 1])
        b1_cols = sb("b1_cols", [P, NF])
        b2_row = sb("b2_row", [1, D])
        col_minus_row = sb("col_minus_row", [P, S], I32)
        slot_iota = sb("slot_iota", [P, B, SLOTS], I32)
        slot_of_batch = sb("slot_of_batch", [P, B, SLOTS])
        same_batch = sb("same_batch", [P, SLOTS])
        warm = sb("warm", [P, 2 * S], mybir.dt.bfloat16)
        ident = sb("ident", [P, P])
        earlier = sb("earlier", [P, NJ, S])
        ones = sb("ones", [P, P])
        minus_half = sb("minus_half", [P, NT])
        at_least = sb("at_least", [P, E + 1, NT])
        mask = sb("mask", [P, E, NT])
        w_hi = sb("w_hi", [P, E, NK, D], F32R)
        w_lo = sb("w_lo", [P, E, NK, D], F32R)
        stats = sb("stats", [P, NT, 6])
        mean_var = sb("mean_var", [P, NT, 2])
        var_eps = sb("var_eps", [P, NT])
        rstd = sb("rstd", [P, NT])
        minus_mean = sb("minus_mean", [P, NT])
        xn = sb("xn", [P, NJ, D])
        xT_hi = sb("xT_hi", [P, B, NK, S], F32R)
        xT_lo = sb("xT_lo", [P, B, NK, S], F32R)
        silu = sb("silu", [P, 2, NK, S])
        gu = sb("gu", [P, E, NK, S])
        gu_hi = sb("gu_hi", [P, E, NK, S], F32R)
        gu_lo = sb("gu_lo", [P, E, NK, S], F32R)
        x1 = sb("x1", [P, NT, D])
        stats2 = sb("stats2", [P, NJ, 6])
        mean_var2 = sb("mean_var2", [P, NJ, 2])
        var_eps2 = sb("var_eps2", [P, NJ])
        rstd2 = sb("rstd2", [P, NJ])
        minus_mean2 = sb("minus_mean2", [P, NJ])
        xn2 = sb("xn2", [P, NT, D])
        base = sb("base", [P, NT, D])
        product = sb("product", [P, NJ, D])
        logits = sb("logits", [P, NT])
        diag = sb("diag", [P, NJ, P])
        above = sb("above", [P, NT])
        tied = sb("tied", [P, NT])
        scratch_above = sb("scratch_above", [P, NJ, S])
        scratch_tied = sb("scratch_tied", [P, NJ, S])
        select = sb("select", [P, NT, SLOTS])
        top_logit = sb("top_logit", [P, B])
        shift_row = sb("shift_row", [P, NT, 2])
        token_row = sb("token_row", [P, NT], I32)
        expo = sb("expo", [P, 1])
        expo_inv = sb("expo_inv", [P, 1])
        weight = sb("weight", [P, 1])
        fxT = sb("fxT", [P, NK, SLOTS])
        gT = sb("gT", [P, NF, SLOTS])
        base_slots = sb("base_slots", [P, D])
        slot_rows = sb("slot_rows", [P, D])
        row_index = sb("row_index", [P, 1], mybir.dt.uint32)

        h_ps = [psum(f"h_ps{i}", [P, NK, S]) for i in range(2)]
        y_ps = [psum(f"y_ps{i}", [P, NJ, D]) for i in range(2)]
        xT_ps = psum("xT_ps", [P, NK, S])
        logit_ps = psum("logit_ps", [P, 2 * S])
        fx_ps = psum("fx_ps", [P, 2 * S])
        fxT_ps = fx_ps[:, 0:NK * SLOTS].rearrange("p (k s) -> p k s", k=NK)
        slots_ps = psum("slots_ps", [P, 2 * S])
        shift_ps = xT_ps[:, 0, 0:2]
        base_ps = slots_ps[:, 0:D]
        ffn_ps = logit_ps[:, 0:D]
        sum_ps = logit_ps[:, D:D + 1]

        d_x = [sem(f"d_x{b}") for b in range(B)]
        d_tok = sem("d_tok")
        d_wT = [sem(f"d_wT{e}") for e in range(E)]
        d_wr = sem("d_wr")
        d_b = sem("d_b")
        d_w1 = sem("d_w1")
        d_w2 = sem("d_w2")
        d_out = sem("d_out")
        s_iota = sem("s_iota")
        s_const = sem("s_const")
        s_half = sem("s_half")
        s_geq = sem("s_geq")
        s_mask = sem("s_mask")
        s_whi = sem("s_whi")
        s_wlo = [sem(f"s_wlo{e}") for e in range(E)]
        s_stats = sem("s_stats")
        s_mean = sem("s_mean")
        s_veps = sem("s_veps")
        s_rstd = sem("s_rstd")
        s_xn = sem("s_xn")
        s_xTps = sem("s_xTps")
        s_xhi = sem("s_xhi")
        s_xlo = sem("s_xlo")
        s_h = sem("s_h")
        s_silu = sem("s_silu")
        s_gu = sem("s_gu")
        s_ghi = sem("s_ghi")
        s_glo = sem("s_glo")
        s_y = sem("s_y")
        s_x1 = sem("s_x1")
        s_stats2 = sem("s_stats2")
        s_mean2 = sem("s_mean2")
        s_veps2 = sem("s_veps2")
        s_rstd2 = sem("s_rstd2")
        s_xn2 = sem("s_xn2")
        s_base = sem("s_base")
        s_logit = sem("s_logit")
        s_diag = sem("s_diag")
        s_lrow = sem("s_lrow")
        s_count = sem("s_count")
        s_top = sem("s_top")
        s_select = sem("s_select")
        s_gather = sem("s_gather")
        s_fx = sem("s_fx")
        s_shift = sem("s_shift")
        s_exp = sem("s_exp")
        s_sum = sem("s_sum")
        s_einv = sem("s_einv")
        s_weight = sem("s_weight")
        s_bslots = sem("s_bslots")
        s_bcopy = sem("s_bcopy")
        s_index = sem("s_index")
        s_rows = sem("s_rows")
        s_trow = sem("s_trow")
        d_scatter = sem("d_scatter")
        s_hid = sem("s_hid")
        s_g = sem("s_g")
        s_ffn = sem("s_ffn")
        s_warm = sem("s_warm")
        s_slots = sem("s_slots")
        s_same = sem("s_same")
        s_same0 = sem("s_same0")
        s_mmean = sem("s_mmean")
        s_mmean2 = sem("s_mmean2")
        s_gathered = sem("s_gathered")
        s_shifted = sem("s_shifted")

        def wait(eng, semaphore, value):
            if not isinstance(value, int) or value > 0:
                eng.wait_ge(semaphore, value)

        block = ctx.enter_context(nc.Block())

        @block.sync
        def _(sp):
            sp.dma_start(x_in[:, 0:NJ, :], x_tiles[:, 0:NJ, :]).then_inc(d_x[0], 16)
            sp.dma_start(wT_in[:, 1], wT_tiles[1]).then_inc(d_wT[1], 16)
            sp.dma_start(tok[:, :], tokens).then_inc(d_tok, 16)
            sp.dma_start(x_in[:, NJ:2 * NJ, :], x_tiles[:, NJ:2 * NJ, :]).then_inc(d_x[1], 16)
            sp.dma_start(wT_in[:, 3], wT_tiles[3]).then_inc(d_wT[3], 16)
            sp.dma_start(br_all[:, :], br.partition_broadcast(P)).then_inc(d_wr, 16)
            sp.dma_start(wr_all[:, :], wr.partition_broadcast(P)).then_inc(d_wr, 16)
            for b in range(2, B):
                sp.dma_start(x_in[:, NJ * b:NJ * b + NJ, :], x_tiles[:, NJ * b:NJ * b + NJ, :]).then_inc(d_x[b], 16)
            sp.dma_start(b1_cols[:, :], b1).then_inc(d_b, 16)
            sp.dma_start(b2_row[:, :], b2).then_inc(d_b, 16)
            sp.dma_start(w1_in[:, :, :], w1_tiles).then_inc(d_w1, 16)
            sp.dma_start(w2_in[:, :, :], w2_tiles).then_inc(d_w2, 16)
            for b in range(B):
                sp.wait_ge(s_base, b + 1)
                sp.dma_start(out_tiles[:, NJ * b:NJ * b + NJ, :], base[:, NJ * b:NJ * b + NJ, :]).then_inc(d_out, 16)
            sp.wait_ge(d_out, 16 * B)

        @block.tensor
        def _(pe):
            def transpose_xn(b):
                pe.wait_ge(s_xn, b + 1)
                wait(pe, s_xlo, b)
                for k in range(NK):
                    for j in range(NJ):
                        mm = pe.transpose(xT_ps[:, k, P * j:P * j + P], xn[:, j, P * k:P * k + P], ident[:, :])
                mm.then_inc(s_xTps, 1)

            def layer1(b, e):
                u = E * b + e
                pe.wait_ge(s_xhi, b + 1)
                if b == 0:
                    pe.wait_ge(s_wlo[e], 1)
                wait(pe, s_gu, u - 1)
                for f in range(NK):
                    rows = slice(P * f, P * f + P)
                    for w, v in ((w_hi, xT_hi), (w_lo, xT_hi), (w_hi, xT_lo)):
                        if v is xT_lo:
                            pe.wait_ge(s_xlo, b + 1)
                        for k in range(NK):
                            mm = pe.matmul(h_ps[e % 2][:, f, :], w[:, e, k, rows], v[:, b, k, :],
                                           start=(w is w_hi and v is xT_hi and k == 0),
                                           stop=(v is xT_lo and k == NK - 1))
                mm.then_inc(s_h, 1)

            def layer2(b, e):
                u = E * b + e
                pe.wait_ge(s_ghi, u + 1)
                wait(pe, s_x1, NJ * (u - 1))
                for j in range(NJ):
                    cols = slice(P * j, P * j + P)
                    for g, w in ((gu_hi, w_hi), (gu_hi, w_lo), (gu_lo, w_hi)):
                        if g is gu_lo:
                            pe.wait_ge(s_glo, u + 1)
                        for k in range(NK):
                            mm = pe.matmul(y_ps[e % 2][:, j, :], g[:, e, k, cols], w[:, e, k, :],
                                           start=(g is gu_hi and w is w_hi and k == 0),
                                           stop=(g is gu_lo and k == NK - 1))
                mm.then_inc(s_y, 1)

            def logit_row(b):
                pe.wait_ge(s_diag, NJ * (b + 1))
                wait(pe, s_top, b)
                for j in range(NJ):
                    mm = pe.matmul(logit_ps[:, P * j:P * j + P], ones[:, :], diag[:, j, :], start=True, stop=True)
                mm.then_inc(s_lrow, 1)

            def gather(b):
                pe.wait_ge(s_select, b + 1)
                for k in range(NK):
                    for j in range(NJ):
                        t = NJ * b + j
                        mm = pe.matmul(fxT_ps[:, k, :], xn2[:, t, P * k:P * k + P], select[:, t, :],
                                       start=(b == 0 and k == 0 and j == 0), stop=False, skip_group_check=True)
                mm.then_inc(s_gather, 1)
                pe.wait_ge(s_shift, b + 1)
                for j in range(NJ):
                    t = NJ * b + j
                    mm = pe.matmul(shift_ps, select[:, t, :], shift_row[:, t, :], start=(b == 0 and j == 0),
                                   stop=False, skip_group_check=True)
                mm.then_inc(s_shifted, 1)

            def gather_base(b):
                pe.wait_ge(s_base, b + 1)
                for j in range(NJ):
                    t = NJ * b + j
                    mm = pe.matmul(base_ps, select[:, t, :], base[:, t, :], start=(t == 0), stop=(t == NT - 1))
                mm.then_inc(s_bslots, 1)

            def keep_warm(n, bank):
                for _ in range(n):
                    pe.matmul(bank[:, :, :], warm[:, 0:P], warm[:, :], start=True, stop=True)

            def batch(b, first=False, last=False):
                if not (first or last):
                    transpose_xn(b + 1)
                layer1(b, 2)
                if first or last:
                    layer1(b, 3)
                layer2(b, 0)
                if first:
                    transpose_xn(b + 1)
                if not (first or last):
                    layer1(b, 3)
                layer2(b, 1)
                if not last:
                    layer1(b + 1, 0)
                    if not first:
                        logit_row(b - 1)
                layer2(b, 2)
                if not last:
                    layer1(b + 1, 1)
                else:
                    logit_row(b - 1)
                layer2(b, 3)

            pe.wait_ge(s_warm, 1)
            keep_warm(WARM_START, xT_ps)
            pe.wait_ge(s_const, 2)
            transpose_xn(0)
            keep_warm(WARM_LAYER1, h_ps[1])
            layer1(0, 0)
            layer1(0, 1)
            batch(0, first=True)
            for b in range(1, B - 1):
                batch(b)
            batch(B - 1, last=True)
            gather(0)
            gather_base(0)
            gather(1)
            gather_base(1)
            gather(2)
            logit_row(B - 1)
            gather_base(2)
            gather(B - 1)
            gather_base(B - 1)

            hid = (fx_ps[:, 0:SLOTS], h_ps[0][:, 0, 0:SLOTS], h_ps[1][:, 0, 0:SLOTS], y_ps[0][:, 0, 0:SLOTS])
            pe.wait_ge(s_fx, 1)
            pe.wait_ge(d_w1, 16)
            pe.wait_ge(d_w2, 16)
            pe.wait_ge(d_b, 32)

            def ffn_in(f):
                for k in range(NK):
                    mm = pe.matmul(hid[f % 4], w1_in[:, k, P * f:P * f + P], fxT[:, k, :],
                                   start=(k == 0), stop=(k == NK - 1))
                mm.then_inc(s_hid, 1)

            def ffn_out(f):
                pe.wait_ge(s_g, f + 1)
                return pe.matmul(ffn_ps, gT[:, f, :], w2_in[:, f, :], start=False, stop=(f == NF - 1))

            ffn_in(0)
            pe.wait_ge(s_exp, 1)
            pe.wait_ge(s_same, 1)
            pe.wait_ge(s_top, B)
            pe.matmul(sum_ps, same_batch[:, :], expo[:, :], start=True, stop=True).then_inc(s_sum, 1)
            for f in range(1, 4):
                ffn_in(f)
            pe.wait_ge(s_einv, 1)
            pe.matmul(ffn_ps, ones[0:1, :], b2_row[:, :], start=True, stop=False)
            for f in range(4, NF):
                ffn_out(f - 4)
                ffn_in(f)
            for f in range(NF - 4, NF):
                mm = ffn_out(f)
            mm.then_inc(s_ffn, 1)

        @block.scalar
        def _(act):
            act.dma_start(wT_in[:, 0], wT_tiles[0]).then_inc(d_wT[0], 16)
            act.dma_start(wT_in[:, 2], wT_tiles[2]).then_inc(d_wT[2], 16)
            act.preload_act_table(ACT.Silu)

            def split_w(e):
                act.wait_ge(d_wT[e], 16)
                act.activation(w_hi[:, e], wT_in[:, e], ACT.Copy).then_inc(s_whi, 1)

            def split_x(b):
                act.wait_ge(s_xTps, b + 1)
                act.activation(xT_hi[:, b], xT_ps[:, :, :], ACT.Copy).then_inc(s_xhi, 1)

            def normalise_x(b):
                act.wait_ge(s_mmean, b)
                act.wait_ge(s_xTps, b)
                for j in range(NJ):
                    t = NJ * b + j
                    n = act.activation(xn[:, j, :], x_in[:, t, :], ACT.Identity, bias=minus_mean[:, t:t + 1],
                                       scale=rstd[:, t:t + 1])
                n.then_inc(s_xn, 1)

            def normalise_x1(b):
                act.wait_ge(s_mmean2, b + 1)
                for j in range(NJ):
                    t = NJ * b + j
                    n = act.activation(xn2[:, t, :], x1[:, t, :], ACT.Identity, bias=minus_mean2[:, j:j + 1],
                                       scale=rstd2[:, j:j + 1])
                n.then_inc(s_xn2, 1)

            def gate(b, e):
                u = E * b + e
                act.wait_ge(s_h, u + 1)
                wait(act, s_gu, u - 1)
                act.activation(silu[:, e % 2], h_ps[e % 2][:, :, :], ACT.Silu).then_inc(s_silu, 1)

            def high_part(b, e):
                act.wait_ge(s_gu, E * b + e + 1)
                act.activation(gu_hi[:, e], gu[:, e], ACT.Copy).then_inc(s_ghi, 1)

            def diagonal(b):
                wait(act, s_lrow, b)
                for j in range(NJ):
                    t = NJ * b + j
                    act.wait_ge(s_logit, t + 1)
                    act.activation(diag[:, j, :], ident[:, :], ACT.Copy, scale=logits[:, t:t + 1]).then_inc(s_diag, 1)

            def batch(b, first=False, last=False, more=False):
                if not (first or last):
                    split_x(b + 1)
                gate(b, 2)
                high_part(b, 2)
                if not (first or last):
                    normalise_x1(b - 1)
                gate(b, 3)
                if first:
                    split_x(b + 1)
                if last:
                    normalise_x1(b - 1)
                high_part(b, 3)
                if not first:
                    diagonal(b - 1)
                if more:
                    normalise_x(b + 2)
                if not last:
                    gate(b + 1, 0)
                    high_part(b + 1, 0)
                    gate(b + 1, 1)
                    high_part(b + 1, 1)

            split_w(0)
            split_w(1)
            split_x(0)
            split_w(2)
            split_w(3)
            gate(0, 0)
            high_part(0, 0)
            gate(0, 1)
            normalise_x(1)
            high_part(0, 1)
            batch(0, first=True, more=True)
            for b in range(1, B - 1):
                batch(b, more=(b < B - 2))
            batch(B - 1, last=True)
            act.preload_act_table(ACT.Exp)
            diagonal(B - 1)
            act.wait_ge(s_shifted, B)
            act.activation(expo[:, :], shift_ps[:, 0:1], ACT.Exp).then_inc(s_exp, 1)
            act.preload_act_table(ACT.Gelu)
            hid = (fx_ps[:, 0:SLOTS], h_ps[0][:, 0, 0:SLOTS], h_ps[1][:, 0, 0:SLOTS], y_ps[0][:, 0, 0:SLOTS])
            act.wait_ge(d_b, 32)
            for f in range(NF):
                act.wait_ge(s_hid, f + 1)
                act.activation(gT[:, f, :], hid[f % 4], ACT.Gelu, bias=b1_cols[:, f:f + 1]).then_inc(s_g, 1)
        @block.gpsimd
        def _(pool):
            pool.iota(col_minus_row[:, :], [[1, S]], base=0, channel_multiplier=-1).then_inc(s_iota, 1)
            pool.memset(minus_half[:, :], -0.5).then_inc(s_half, 1)
            pool.iota(slot_iota[:, :, :], [[-TOP, B], [1, SLOTS]], base=0, channel_multiplier=0).then_inc(s_iota, 1)
            pool.iota(token_row[:, :], [[P, NT]], base=0, channel_multiplier=1).then_inc(s_trow, 1)

            def inverse_root(variance, shifted_var, target, shifted_signal, signal, count):
                pool.tensor_scalar(shifted_var, variance, EPS, None, ALU.add).then_inc(shifted_signal, 1)
                pool.wait_ge(shifted_signal, count)
                pool.tensor_tensor(target, shifted_var, minus_half[:, 0:target.shape[1]], ALU.pow).then_inc(signal, 1)

            def rstd_x(b):
                tiles = slice(NJ * b, NJ * b + NJ)
                pool.wait_ge(s_mean, b + 1)
                inverse_root(mean_var[:, tiles, 1], var_eps[:, tiles], rstd[:, tiles], s_veps, s_rstd, b + 1)

            def rstd_x1(b):
                pool.wait_ge(s_mean2, b + 1)
                wait(pool, s_xn2, b)
                inverse_root(mean_var2[:, :, 1], var_eps2[:, :], rstd2[:, :], s_veps2, s_rstd2, b + 1)

            def split_w(e):
                pool.wait_ge(s_whi, e + 1)
                pool.tensor_tensor(w_lo[:, e], wT_in[:, e], w_hi[:, e].bitcast(F32), ALU.subtract).then_inc(s_wlo[e], 1)

            def low_part(b, e):
                u = E * b + e
                pool.wait_ge(s_ghi, u + 1)
                pool.tensor_tensor(gu_lo[:, e], gu[:, e], gu_hi[:, e].bitcast(F32),
                                   ALU.subtract).then_inc(s_glo, 1)

            def add_base(b):
                pool.wait_ge(s_xn2, b + 1)
                pool.tensor_tensor(base[:, NJ * b:NJ * b + NJ, :], x1[:, NJ * b:NJ * b + NJ, :],
                                   xn2[:, NJ * b:NJ * b + NJ, :],
                                   ALU.add).then_inc(s_base, 1)

            def batch(b, first=False, last=False):
                if not first:
                    rstd_x1(b - 1)
                low_part(b, 2)
                low_part(b, 3)
                if first:
                    rstd_x(3)
                if not first:
                    add_base(b - 1)
                if not last:
                    low_part(b + 1, 0)
                    low_part(b + 1, 1)

            pool.wait_ge(s_half, 1)
            rstd_x(0)
            split_w(0)
            split_w(2)
            rstd_x(1)
            low_part(0, 0)
            rstd_x(2)
            low_part(0, 1)
            batch(0, first=True)
            for b in range(1, B - 1):
                batch(b)
            batch(B - 1, last=True)
            rstd_x1(B - 1)
            add_base(B - 1)
            pool.wait_ge(s_index, 1)
            pool.wait_ge(d_out, 16 * B)
            pool.wait_ge(s_rows, 1)
            pool.indirect_dma_start(out.rearrange("b s d -> (b s) d"), bass.IndirectOffsetOnAxis(row_index[:, 0:1], 0),
                                    slot_rows[:, :], None).then_inc(d_scatter, 16)
            pool.wait_ge(d_scatter, 16)

        @block.vector
        def _(dve):
            def statistics(source, st, mv, tiles, signal_st, count, signal):
                for j, t in enumerate(tiles):
                    dve.bn_stats(st[:, j, :], source[:, t, :]).then_inc(signal_st, 1)
                dve.wait_ge(signal_st, count)
                for j, t in enumerate(tiles):
                    aggr = dve.bn_aggr(mv[:, j, :], st[:, j, :])
                aggr.then_inc(signal, 1)

            def stats_x1(b):
                wait(dve, s_mean2, b)
                wait(dve, s_xn2, b)
                wait(dve, s_veps2, b)
                dve.wait_ge(s_x1, NJ * E * (b + 1))
                statistics(x1, stats2, mean_var2, [NJ * b + j for j in range(NJ)], s_stats2, NJ * b + NJ, s_mean2)

            def normalise_x(b):
                dve.wait_ge(s_rstd, 1)
                for j in range(NJ):
                    t = NJ * b + j
                    n = dve.tensor_scalar(xn[:, j, :], x_in[:, t, :], mean_var[:, t, 0:1], rstd[:, t:t + 1],
                                          ALU.subtract, ALU.mult)
                n.then_inc(s_xn, 1)

            def normalise_x1(b):
                dve.wait_ge(s_rstd2, b + 1)
                for j in range(NJ):
                    t = NJ * b + j
                    n = dve.tensor_scalar(xn2[:, t, :], x1[:, t, :], mean_var2[:, j, 0:1], rstd2[:, j:j + 1],
                                          ALU.subtract, ALU.mult)
                n.then_inc(s_xn2, 1)

            def router(b):
                dve.wait_ge(s_xn2, b + 1)
                wait(dve, s_logit, NJ * b)
                for j in range(NJ):
                    t = NJ * b + j
                    dve.tensor_tensor_reduce(product[:, j, :], xn2[:, t, :], wr_all[:, :], 1.0, br_all[:, 0:1],
                                             ALU.mult, ALU.add, logits[:, t:t + 1]).then_inc(s_logit, 1)

            def split_x(b):
                dve.wait_ge(s_xhi, b + 1)
                dve.tensor_tensor(xT_lo[:, b], xT_ps[:, :, :], xT_hi[:, b].bitcast(F32), ALU.subtract).then_inc(s_xlo, 1)

            def gate(b, e):
                u = E * b + e
                dve.wait_ge(s_silu, u + 1)
                wait(dve, s_glo, u - E + 1)
                dve.tensor_tensor(gu[:, e], silu[:, e % 2], h_ps[e % 2][:, :, :], ALU.mult).then_inc(s_gu, 1)

            def accumulate(b, e):
                u = E * b + e
                dve.wait_ge(s_y, u + 1)
                for j in range(NJ):
                    t = NJ * b + j
                    if e > 0:
                        dve.wait_ge(s_x1, NJ * (u - 1) + j + 1)
                    dve.scalar_tensor_tensor(out=x1[:, t, :], in0=y_ps[e % 2][:, j, :], scalar=mask[:, e, t:t + 1],
                                             in1=(x_in if e == 0 else x1)[:, t, :], op0=ALU.mult,
                                             op1=ALU.add).then_inc(s_x1, 1)

            def count(b):
                dve.wait_ge(s_lrow, b + 1)
                wait(dve, s_count, 2 * NJ * b)
                for j in range(NJ):
                    t = NJ * b + j
                    n = P * (j + 1)
                    dve.tensor_scalar(scratch_above[:, j, :], logit_ps[:, 0:S], logits[:, t:t + 1], 0.0, ALU.is_gt,
                                      ALU.add, accum_out=above[:, t:t + 1]).then_inc(s_count, 1)
                    dve.scalar_tensor_tensor(out=scratch_tied[:, j, 0:n], in0=logit_ps[:, 0:n],
                                             scalar=logits[:, t:t + 1], in1=earlier[:, j, 0:n], op0=ALU.is_equal,
                                             op1=ALU.mult, accum_out=tied[:, t:t + 1]).then_inc(s_count, 1)
                dve.reduce_max(top_logit[:, b:b + 1], logit_ps[:, 0:S], AX_X).then_inc(s_top, 1)

            def choose(b):
                dve.wait_ge(s_count, 2 * NJ * (b + 1))
                for j in range(NJ):
                    t = NJ * b + j
                    s = dve.tensor_scalar(select[:, t, :], slot_of_batch[:, b, :], above[:, t:t + 1],
                                          tied[:, t:t + 1], ALU.subtract, ALU.is_equal)
                s.then_inc(s_select, 1)
                dve.wait_ge(s_top, b + 1)
                dve.tensor_scalar(shift_row[:, NJ * b:NJ * b + NJ, 0], logits[:, NJ * b:NJ * b + NJ],
                                  top_logit[:, b:b + 1], None, ALU.subtract).then_inc(s_shift, 1)

            def split_w(e):
                dve.wait_ge(s_whi, e + 1)
                dve.tensor_tensor(w_lo[:, e], wT_in[:, e], w_hi[:, e].bitcast(F32), ALU.subtract).then_inc(s_wlo[e], 1)

            def stats_x(b):
                dve.wait_ge(d_x[b], 16)
                tiles = slice(NJ * b, NJ * b + NJ)
                statistics(x_in, stats[:, tiles, :], mean_var[:, tiles, :], range(NT)[tiles], s_stats, NJ * b + NJ,
                           s_mean)

            def scale_mean(b):
                tiles = slice(NJ * b, NJ * b + NJ)
                dve.wait_ge(s_rstd, b + 1)
                dve.scalar_tensor_tensor(out=minus_mean[:, tiles], in0=mean_var[:, tiles, 0], scalar=-1.0,
                                         in1=rstd[:, tiles], op0=ALU.mult, op1=ALU.mult).then_inc(s_mmean, 1)

            def scale_mean2(b):
                dve.wait_ge(s_rstd2, b + 1)
                dve.scalar_tensor_tensor(out=minus_mean2[:, :], in0=mean_var2[:, :, 0], scalar=-1.0,
                                         in1=rstd2[:, :], op0=ALU.mult, op1=ALU.mult).then_inc(s_mmean2, 1)

            def batch(b, first=False, last=False):
                if not first:
                    stats_x1(b - 1)
                gate(b, 2)
                if not first:
                    scale_mean2(b - 1)
                if first or last:
                    gate(b, 3)
                if first:
                    stats_x(3)
                accumulate(b, 0)
                if not last:
                    split_x(b + 1)
                if not first:
                    router(b - 1)
                if not (first or last):
                    gate(b, 3)
                accumulate(b, 1)
                if first:
                    scale_mean(3)
                if not first and b > 1:
                    choose(b - 2)
                if not last:
                    gate(b + 1, 0)
                if last:
                    accumulate(b, 2)
                if not first:
                    count(b - 1)
                if not last:
                    accumulate(b, 2)
                    gate(b + 1, 1)
                accumulate(b, 3)

            dve.memset(warm[:, :], 0.0).then_inc(s_warm, 1)
            dve.memset(ones[:, :], 1.0).then_inc(s_const, 1)
            dve.memset(same_batch[:, :], 0.0).then_inc(s_same0, 1)
            dve.memset(at_least[:, 0, :], 1.0).then_inc(s_geq, 1)
            dve.memset(at_least[:, E, :], 0.0).then_inc(s_geq, 1)
            dve.wait_ge(s_same0, 1)
            for b in range(B):
                m = dve.memset(same_batch[TOP * b:TOP * b + TOP, TOP * b:TOP * b + TOP], 1.0)
            m.then_inc(s_same, 1)
            dve.wait_ge(s_iota, 1)
            dve.tensor_scalar(ident[:, :], col_minus_row[:, 0:P], 0.0, None, ALU.is_equal).then_inc(s_const, 1)
            dve.tensor_scalar(earlier[:, 0, :], col_minus_row[:, :], 0.0, None, ALU.is_lt).then_inc(s_const, 1)
            dve.tensor_scalar(earlier[:, 1, :], col_minus_row[:, :], float(P), None, ALU.is_lt).then_inc(s_const, 1)
            dve.wait_ge(s_iota, 2)
            dve.tensor_scalar(slot_of_batch[:, :, :], slot_iota[:, :, :], float(TOP), NOT_CHOSEN, ALU.is_ge,
                              ALU.mult).then_inc(s_slots, 1)
            stats_x(0)
            dve.wait_ge(s_slots, 1)
            dve.tensor_tensor(slot_of_batch[:, :, :], slot_of_batch[:, :, :], slot_iota[:, :, :],
                              ALU.add).then_inc(s_slots, 1)
            normalise_x(0)
            dve.wait_ge(d_tok, 16)
            for e in range(1, E):
                dve.tensor_scalar(at_least[:, e, :], tok[:, :], float(e * PER_EXPERT), None,
                                  ALU.is_ge).then_inc(s_geq, 1)
            dve.wait_ge(s_geq, E + 1)
            dve.tensor_tensor(mask[:, :, :], at_least[:, 0:E, :], at_least[:, 1:E + 1, :],
                              ALU.subtract).then_inc(s_mask, 1)
            split_w(1)
            split_x(0)
            stats_x(1)
            split_w(3)
            gate(0, 0)
            scale_mean(1)
            stats_x(2)
            gate(0, 1)
            scale_mean(2)
            dve.wait_ge(s_mask, 1)
            batch(0, first=True)
            dve.wait_ge(s_trow, 1)
            dve.tensor_copy(shift_row[:, :, 1], token_row[:, :])
            dve.wait_ge(d_wr, 32)
            dve.wait_ge(s_slots, 2)
            dve.wait_ge(s_const, 4)
            for b in range(1, B - 1):
                batch(b)
            batch(B - 1, last=True)
            stats_x1(B - 1)
            choose(B - 2)
            normalise_x1(B - 1)
            router(B - 1)
            count(B - 1)
            choose(B - 1)
            dve.wait_ge(s_gather, B)
            dve.tensor_copy(fxT[:, :, :], fxT_ps).then_inc(s_fx, 1)
            dve.wait_ge(s_exp, 1)
            dve.tensor_copy(row_index[:, :], shift_ps[:, 1:2]).then_inc(s_index, 1)
            dve.wait_ge(s_sum, 1)
            dve.reciprocal(expo_inv[:, :], sum_ps).then_inc(s_einv, 1)
            dve.wait_ge(s_einv, 1)
            dve.tensor_tensor(weight[:, :], expo[:, :], expo_inv[:, :], ALU.mult).then_inc(s_weight, 1)
            dve.wait_ge(s_bslots, B)
            dve.tensor_copy(base_slots[:, :], base_ps).then_inc(s_bcopy, 1)
            dve.wait_ge(s_weight, 1)
            dve.wait_ge(s_bcopy, 1)
            dve.wait_ge(s_ffn, 1)
            dve.scalar_tensor_tensor(out=slot_rows[:, :], in0=ffn_ps, scalar=weight[:, 0:1], in1=base_slots[:, :],
                                     op0=ALU.mult, op1=ALU.add).then_inc(s_rows, 1)


def kernel(x, itok_BxS_13_99985, ctx_2048, L0_ffn_Wr, L0_ffn_br, L0_ffn_W1, L0_ffn_b1, L0_ffn_W2, L0_ffn_b2):
    import numpy as np
    import concourse.bacc as bacc
    from concourse.bass_utils import run_bass_kernel_spmd

    B, S, D = x.shape
    flat = np.ascontiguousarray
    arrays = {
        "x": flat(x),
        "tokens": flat(np.asarray(itok_BxS_13_99985).reshape(-1, P).T),
        "wT": flat(np.asarray(ctx_2048).transpose(0, 2, 1)),
        "wr": flat(np.asarray(L0_ffn_Wr).reshape(D)),
        "br": flat(L0_ffn_br),
        "w1": flat(L0_ffn_W1),
        "b1": flat(np.asarray(L0_ffn_b1).reshape(-1, P).T),
        "w2": flat(L0_ffn_W2),
        "b2": flat(np.asarray(L0_ffn_b2).reshape(1, D)),
    }
    nc = bacc.Bacc("TRN2", target_bir_lowering=False, num_devices=1)
    args = [nc.dram_tensor(f"in_{n}", a.shape, mybir.dt.from_np(a.dtype), kind="ExternalInput").ap()
            for n, a in arrays.items()]
    args.append(nc.dram_tensor("out", (B, S, D), F32, kind="ExternalOutput").ap())
    fused_layers(nc, *args)
    r = run_bass_kernel_spmd(nc, [{f"in_{n}": a for n, a in arrays.items()}], core_ids=[0])
    return r.results[0]["out"]
```

```python
from contextlib import ExitStack

import concourse.bass as bass
from concourse import mybir

F32 = mybir.dt.float32
F32R = mybir.dt.float32r
I32 = mybir.dt.int32
ALU = mybir.AluOpType
ACT = mybir.ActivationFunctionType
AX_X = mybir.AxisListType.X

P = 128
VOCAB = 12500
EPS = 1e-5
WARM_START = 12
WARM_LAYER1 = 3
W2_PARTS = 4


def fused_layers(nc, x, tokens, wT, wr, br, w1, b1, w2, b2, out):
    B, S, D = x.shape
    E = wT.shape[0]
    DFF = w1.shape[1]
    NK = D // P
    NJ = S // P
    NT = B * NJ
    NF = DFF // P
    TOP = S // 8
    SLOTS = B * TOP
    PER_EXPERT = VOCAB // E
    assert (NK, NJ, SLOTS) == (2, 2, P)

    x_tiles = x.rearrange("b (j p) d -> p (b j) d", p=P)
    out_tiles = out.rearrange("b (j p) d -> p (b j) d", p=P)
    wT_tiles = wT.rearrange("e (k p) r -> e p k r", p=P)
    w1_tiles = w1.rearrange("(k p) f -> p k f", p=P)
    w2_tiles = w2.rearrange("(f p) d -> p f d", p=P)

    with ExitStack() as ctx:
        def sb(name, shape, dt=F32):
            return ctx.enter_context(nc.sbuf_tensor(name, shape, dt))

        def psum(name, shape):
            return ctx.enter_context(nc.psum_tensor(name, shape, F32))

        def sem(name):
            return ctx.enter_context(nc.semaphore(name))

        x_in = sb("x_in", [P, NT, D])
        tok = sb("tok", [P, NT], I32)
        wT_in = sb("wT_in", [P, E, NK, D])
        w1_in = sb("w1_in", [P, NK, DFF])
        w2_in = sb("w2_in", [P, NF, D])
        wr_all = sb("wr_all", [P, D])
        br_all = sb("br_all", [P, 1])
        b1_row = sb("b1_row", [1, DFF])
        b2_all = sb("b2_all", [P, D])
        col_minus_row = sb("col_minus_row", [P, S], I32)
        rank_iota = sb("rank_iota", [P, TOP], I32)
        rank_of_slot = sb("rank_of_slot", [P, TOP])
        same_batch = sb("same_batch", [P, SLOTS])
        warm = sb("warm", [P, 2 * S], mybir.dt.bfloat16)
        ident = sb("ident", [P, P])
        earlier = sb("earlier", [P, NJ, S])
        ones = sb("ones", [P, P])
        minus_half = sb("minus_half", [P, NT])
        at_least = sb("at_least", [P, E + 1, NT])
        mask = sb("mask", [P, E, NT])
        w_hi = sb("w_hi", [P, E, NK, D], F32R)
        w_lo = sb("w_lo", [P, E, NK, D], F32R)
        stats = sb("stats", [P, NT, 6])
        mean_var = sb("mean_var", [P, NT, 2])
        var_eps = sb("var_eps", [P, NT])
        rstd = sb("rstd", [P, NT])
        minus_mean = sb("minus_mean", [P, NT])
        xn = sb("xn", [P, NJ, D])
        xT_hi = sb("xT_hi", [P, B, NK, S], F32R)
        xT_lo = sb("xT_lo", [P, B, NK, S], F32R)
        silu = sb("silu", [P, 2, NK, S])
        gu = sb("gu", [P, E, NK, S])
        gu_hi = sb("gu_hi", [P, E, NK, S], F32R)
        gu_lo = sb("gu_lo", [P, E, NK, S], F32R)
        x1 = sb("x1", [P, NT, D])
        stats2 = sb("stats2", [P, NJ, 6])
        mean_var2 = sb("mean_var2", [P, NJ, 2])
        var_eps2 = sb("var_eps2", [P, NJ])
        rstd2 = sb("rstd2", [P, NJ])
        minus_mean2 = sb("minus_mean2", [P, NJ])
        xn2 = sb("xn2", [P, NT, D])
        base = sb("base", [P, NT, D])
        product = sb("product", [P, NJ, D])
        dots = sb("dots", [P, NJ])
        logits = sb("logits", [P, NT])
        above = sb("above", [P, NT])
        tied = sb("tied", [P, NT])
        scratch_above = sb("scratch_above", [P, NJ, S])
        scratch_tied = sb("scratch_tied", [P, NJ, S])
        select = sb("select", [P, NT, SLOTS])
        top_logit = sb("top_logit", [P, B])
        shift_row = sb("shift_row", [P, NT, 2])
        token_row = sb("token_row", [P, NT], I32)
        expo = sb("expo", [P, 1])
        expo_inv = sb("expo_inv", [P, 1])
        weight = sb("weight", [P, 1])
        fxT = sb("fxT", [P, NK, SLOTS])
        gT = sb("gT", [P, NF, SLOTS])
        gT_hi = sb("gT_hi", [P, NF, SLOTS], F32R)
        gT_lo = sb("gT_lo", [P, NF, SLOTS], F32R)
        w2_hi = sb("w2_hi", [P, NF, D], F32R)
        w2_lo = sb("w2_lo", [P, NF, D], F32R)
        base_slots = sb("base_slots", [P, D])
        slot_rows = sb("slot_rows", [P, D])
        row_index = sb("row_index", [P, 1], mybir.dt.uint32)

        h_ps = [psum(f"h_ps{i}", [P, NK, S]) for i in range(2)]
        y_ps = [psum(f"y_ps{i}", [P, NJ, D]) for i in range(2)]
        xT_ps = psum("xT_ps", [P, NK, S])
        logit_ps = psum("logit_ps", [P, 2 * S])
        fx_ps = psum("fx_ps", [P, 2 * S])
        fxT_ps = fx_ps[:, 0:NK * SLOTS].rearrange("p (k s) -> p k s", k=NK)
        last_row_ps = psum("last_row_ps", [P, 2 * S])
        shift_ps = xT_ps[:, 0, 0:2]
        sum_ps = xT_ps[:, 0, 2:3]
        ffn_ps = logit_ps[:, 0:D]

        def h_bank(b, e):
            u = E * b + e
            return y_ps[1] if u == 2 else h_ps[(u if u < 2 else u + 1) % 2]

        def row_ps(b):
            return logit_ps[:, 0:S] if b < B - 1 else last_row_ps[:, 0:S]

        hid_ps = [bank[:, 0, :].rearrange("p (i s) -> p i s", i=2) for bank in (h_ps[0], y_ps[0], y_ps[1], h_ps[1])]

        d_x = [sem(f"d_x{b}") for b in range(B)]
        d_tok = sem("d_tok")
        d_wT = [sem(f"d_wT{e}") for e in range(E)]
        d_wr = sem("d_wr")
        d_b = sem("d_b")
        d_w1 = sem("d_w1")
        d_w2 = sem("d_w2")
        d_out = sem("d_out")
        s_iota = sem("s_iota")
        s_const = sem("s_const")
        s_half = sem("s_half")
        s_geq = sem("s_geq")
        s_mask = sem("s_mask")
        s_whi = sem("s_whi")
        s_wlo = [sem(f"s_wlo{e}") for e in range(E)]
        s_stats = sem("s_stats")
        s_mean = sem("s_mean")
        s_veps = sem("s_veps")
        s_rstd = sem("s_rstd")
        s_xn = sem("s_xn")
        s_xTps = sem("s_xTps")
        s_xhi = sem("s_xhi")
        s_xlo = sem("s_xlo")
        s_h = sem("s_h")
        s_silu = sem("s_silu")
        s_gu = sem("s_gu")
        s_ghi = sem("s_ghi")
        s_glo = sem("s_glo")
        s_y = sem("s_y")
        s_x1 = sem("s_x1")
        s_stats2 = sem("s_stats2")
        s_mean2 = sem("s_mean2")
        s_veps2 = sem("s_veps2")
        s_rstd2 = sem("s_rstd2")
        s_xn2 = sem("s_xn2")
        s_base = sem("s_base")
        s_logit = sem("s_logit")
        s_dot = sem("s_dot")
        s_lrow = sem("s_lrow")
        s_count = sem("s_count")
        s_top = sem("s_top")
        s_select = sem("s_select")
        s_select_last = sem("s_select_last")
        s_gather = sem("s_gather")
        s_fx = sem("s_fx")
        s_shift = sem("s_shift")
        s_shift_last = sem("s_shift_last")
        s_exp = sem("s_exp")
        s_sum = sem("s_sum")
        s_einv = sem("s_einv")
        s_weight = sem("s_weight")
        d_base = sem("d_base")
        s_bias = sem("s_bias")
        s_index = sem("s_index")
        s_rows = sem("s_rows")
        s_trow = sem("s_trow")
        d_scatter = sem("d_scatter")
        s_hid = sem("s_hid")
        s_g = sem("s_g")
        s_ffn = sem("s_ffn")
        s_gThi = sem("s_gThi")
        s_gTlo = sem("s_gTlo")
        s_w2hi = sem("s_w2hi")
        s_w2lo = sem("s_w2lo")
        s_warm = sem("s_warm")
        s_ranks = sem("s_ranks")
        s_zero = sem("s_zero")
        s_same = sem("s_same")
        s_same0 = sem("s_same0")
        s_mmean = sem("s_mmean")
        s_mmean2 = sem("s_mmean2")
        s_shifted = sem("s_shifted")

        def wait(eng, semaphore, value):
            if not isinstance(value, int) or value > 0:
                eng.wait_ge(semaphore, value)

        block = ctx.enter_context(nc.Block())

        @block.sync
        def _(sp):
            sp.dma_start(x_in[:, 0:NJ, :], x_tiles[:, 0:NJ, :]).then_inc(d_x[0], 16)
            sp.dma_start(wT_in[:, 1], wT_tiles[1]).then_inc(d_wT[1], 16)
            sp.dma_start(tok[:, :], tokens).then_inc(d_tok, 16)
            sp.dma_start(x_in[:, NJ:2 * NJ, :], x_tiles[:, NJ:2 * NJ, :]).then_inc(d_x[1], 16)
            sp.dma_start(wT_in[:, 3], wT_tiles[3]).then_inc(d_wT[3], 16)
            sp.dma_start(br_all[:, :], br.partition_broadcast(P)).then_inc(d_wr, 16)
            sp.dma_start(wr_all[:, :], wr.partition_broadcast(P)).then_inc(d_wr, 16)
            for b in range(2, B):
                sp.dma_start(x_in[:, NJ * b:NJ * b + NJ, :], x_tiles[:, NJ * b:NJ * b + NJ, :]).then_inc(d_x[b], 16)
            sp.dma_start(b1_row[:, :], b1).then_inc(d_b, 16)
            sp.dma_start(b2_all[:, :], b2.partition_broadcast(P)).then_inc(d_b, 16)
            sp.dma_start(w1_in[:, :, :], w1_tiles).then_inc(d_w1, 16)
            sp.dma_start(w2_in[:, :, :], w2_tiles).then_inc(d_w2, 16)
            for b in range(B):
                sp.wait_ge(s_base, b + 1)
                sp.dma_start(out_tiles[:, NJ * b:NJ * b + NJ, :], base[:, NJ * b:NJ * b + NJ, :]).then_inc(d_out, 16)
            sp.wait_ge(d_out, 16 * B)

        @block.tensor
        def _(pe):
            def transpose_xn(b):
                pe.wait_ge(s_xn, b + 1)
                wait(pe, s_xlo, b)
                for k in range(NK):
                    for j in range(NJ):
                        mm = pe.transpose(xT_ps[:, k, P * j:P * j + P], xn[:, j, P * k:P * k + P], ident[:, :])
                mm.then_inc(s_xTps, 1)

            def layer1(b, e):
                u = E * b + e
                pe.wait_ge(s_xhi, b + 1)
                if b == 0:
                    pe.wait_ge(s_wlo[e], 1)
                wait(pe, s_gu, {2: 0, 3: 1}.get(u, u - 1))
                for f in range(NK):
                    rows = slice(P * f, P * f + P)
                    for w, v in ((w_hi, xT_hi), (w_lo, xT_hi), (w_hi, xT_lo)):
                        if v is xT_lo:
                            pe.wait_ge(s_xlo, b + 1)
                        for k in range(NK):
                            mm = pe.matmul(h_bank(b, e)[:, f, :], w[:, e, k, rows], v[:, b, k, :],
                                           start=(w is w_hi and v is xT_hi and k == 0),
                                           stop=(v is xT_lo and k == NK - 1))
                mm.then_inc(s_h, 1)

            def layer2(b, e, last=False):
                u = E * b + e
                pe.wait_ge(s_ghi, u + 1)
                wait(pe, s_x1, NJ * (u - 1))
                if u == 1:
                    pe.wait_ge(s_gu, 3)
                for j in range(NJ):
                    cols = slice(P * j, P * j + P)
                    for g, w in ((gu_hi, w_hi), (gu_hi, w_lo), (gu_lo, w_hi)):
                        if g is gu_lo:
                            pe.wait_ge(s_glo, u + 1)
                        for k in range(NK):
                            bank = h_ps[0] if last and j > 0 else y_ps[e % 2]
                            mm = pe.matmul(bank[:, j, :], g[:, e, k, cols], w[:, e, k, :],
                                           start=(g is gu_hi and w is w_hi and k == 0),
                                           stop=(g is gu_lo and k == NK - 1))
                    if last or j == NJ - 1:
                        mm.then_inc(s_y, 1)

            def logit_row(b):
                pe.wait_ge(s_logit, NJ * (b + 1))
                if b < B - 1:
                    wait(pe, s_top, b)
                for j in range(NJ):
                    t = NJ * b + j
                    mm = pe.matmul(row_ps(b)[:, P * j:P * j + P], logits[:, t:t + 1].to_broadcast([P, P]), ident[:, :],
                                   start=True, stop=True)
                mm.then_inc(s_lrow, 1)

            def gather(b):
                if b < B - 1:
                    pe.wait_ge(s_select, b + 1)
                else:
                    pe.wait_ge(s_select_last, 1)
                pe.wait_ge(s_xn2, b + 1)
                if b == 0:
                    pe.wait_ge(s_zero, 1)
                for k in range(NK):
                    for j in range(NJ):
                        t = NJ * b + j
                        mm = pe.matmul(fxT_ps[:, k, :], xn2[:, t, P * k:P * k + P], select[:, t, :],
                                       start=(b == 0 and k == 0 and j == 0), stop=False, skip_group_check=True)
                mm.then_inc(s_gather, 1)
                if b < B - 1:
                    pe.wait_ge(s_shift, b + 1)
                else:
                    pe.wait_ge(s_shift_last, 1)
                for j in range(NJ):
                    t = NJ * b + j
                    mm = pe.matmul(shift_ps, select[:, t, :], shift_row[:, t, :], start=(b == 0 and j == 0),
                                   stop=False, skip_group_check=True)
                mm.then_inc(s_shifted, 1)

            def keep_warm(n, bank):
                for _ in range(n):
                    pe.matmul(bank[:, :, :], warm[:, 0:P], warm[:, :], start=True, stop=True)

            def batch(b, first=False, last=False):
                if not (first or last):
                    transpose_xn(b + 1)
                layer1(b, 2)
                if first or last:
                    layer1(b, 3)
                layer2(b, 0)
                if first:
                    transpose_xn(b + 1)
                if not (first or last):
                    layer1(b, 3)
                layer2(b, 1)
                if not first:
                    logit_row(b - 1)
                if not last:
                    layer1(b + 1, 0)
                layer2(b, 2)
                if not last:
                    layer1(b + 1, 1)
                layer2(b, 3, last)

            pe.wait_ge(s_warm, 1)
            keep_warm(WARM_START, xT_ps)
            pe.wait_ge(s_const, 2)
            transpose_xn(0)
            keep_warm(WARM_LAYER1, h_ps[1])
            layer1(0, 0)
            layer1(0, 1)
            batch(0, first=True)
            for b in range(1, B - 1):
                batch(b)
            batch(B - 1, last=True)

            def ffn_bias(pair):
                for i in range(2):
                    f = 2 * pair + i
                    pe.matmul(hid_ps[pair][:, i, :], b1_row[:, P * f:P * f + P], ones[0:1, :], start=(i == 0),
                              stop=False, skip_group_check=True)

            def ffn_in(pair):
                for i in range(2):
                    f = 2 * pair + i
                    for k in range(NK):
                        mm = pe.matmul(hid_ps[pair][:, i, :], w1_in[:, k, P * f:P * f + P], fxT[:, k, :],
                                       start=False, stop=(i == 1 and k == NK - 1), skip_group_check=True)
                mm.then_inc(s_hid, 1)

            for b in range(B - 2):
                gather(b)
            pe.wait_ge(d_b, 32)
            pe.wait_ge(s_x1, NT * E)
            ffn_bias(0)
            logit_row(B - 1)
            for pair in range(1, NF // 2):
                ffn_bias(pair)
            gather(B - 2)
            gather(B - 1)
            pe.wait_ge(d_w1, 16)
            pe.wait_ge(s_fx, 1)
            for pair in range(NF // 2):
                ffn_in(pair)
            pe.wait_ge(s_w2lo, W2_PARTS)
            pe.wait_ge(s_count, 2 * NJ * (B - 1))
            pe.wait_ge(s_top, B - 1)
            for f in range(NF):
                for g, w in ((gT_hi, w2_hi), (gT_hi, w2_lo), (gT_lo, w2_hi)):
                    if g is gT_hi:
                        pe.wait_ge(s_gThi, f // 2 + 1)
                    else:
                        pe.wait_ge(s_gTlo, f // 2 + 1)
                    mm = pe.matmul(ffn_ps, g[:, f, :], w[:, f, :], start=(f == 0 and g is gT_hi and w is w2_hi),
                                   stop=(f == NF - 1 and g is gT_lo))
                if f == 0:
                    pe.wait_ge(s_exp, 1)
                    pe.wait_ge(s_index, 1)
                    pe.wait_ge(s_same, 1)
                    pe.matmul(sum_ps, same_batch[:, :], expo[:, :], start=True, stop=True).then_inc(s_sum, 1)
            mm.then_inc(s_ffn, 1)

        @block.scalar
        def _(act):
            act.dma_start(wT_in[:, 0], wT_tiles[0]).then_inc(d_wT[0], 16)
            act.dma_start(wT_in[:, 2], wT_tiles[2]).then_inc(d_wT[2], 16)
            act.preload_act_table(ACT.Silu)

            def split_w(e):
                act.wait_ge(d_wT[e], 16)
                act.activation(w_hi[:, e], wT_in[:, e], ACT.Copy).then_inc(s_whi, 1)

            def split_x(b):
                act.wait_ge(s_xTps, b + 1)
                act.activation(xT_hi[:, b], xT_ps[:, :, :], ACT.Copy).then_inc(s_xhi, 1)

            def split_w2(part):
                act.wait_ge(d_w2, 16)
                tiles = slice(NF // W2_PARTS * part, NF // W2_PARTS * (part + 1))
                act.activation(w2_hi[:, tiles], w2_in[:, tiles], ACT.Copy).then_inc(s_w2hi, 1)

            def normalise_x(b):
                act.wait_ge(s_mmean, b)
                act.wait_ge(s_xTps, b)
                for j in range(NJ):
                    t = NJ * b + j
                    n = act.activation(xn[:, j, :], x_in[:, t, :], ACT.Identity, bias=minus_mean[:, t:t + 1],
                                       scale=rstd[:, t:t + 1])
                n.then_inc(s_xn, 1)

            def normalise_x1(b):
                act.wait_ge(s_mmean2, b + 1)
                for j in range(NJ):
                    t = NJ * b + j
                    n = act.activation(xn2[:, t, :], x1[:, t, :], ACT.Identity, bias=minus_mean2[:, j:j + 1],
                                       scale=rstd2[:, j:j + 1])
                n.then_inc(s_xn2, 1)

            def gate(b, e):
                u = E * b + e
                act.wait_ge(s_h, u + 1)
                wait(act, s_gu, u - 1)
                act.activation(silu[:, e % 2], h_bank(b, e)[:, :, :], ACT.Silu).then_inc(s_silu, 1)

            def high_part(b, e):
                act.wait_ge(s_gu, E * b + e + 1)
                wait(act, s_y, E * b + e - E + 1)
                act.activation(gu_hi[:, e], gu[:, e], ACT.Copy).then_inc(s_ghi, 1)

            def batch(b, first=False, last=False, more=False):
                if not (first or last):
                    split_x(b + 1)
                gate(b, 2)
                if first:
                    high_part(b, 1)
                    normalise_x(1)
                high_part(b, 2)
                if not (first or last):
                    split_w2(b)
                    normalise_x1(b - 1)
                gate(b, 3)
                if first:
                    split_x(b + 1)
                if last:
                    normalise_x1(b - 1)
                high_part(b, 3)
                if more:
                    normalise_x(b + 2)
                if first or last:
                    split_w2(b)
                if not last:
                    gate(b + 1, 0)
                    high_part(b + 1, 0)
                    gate(b + 1, 1)
                    high_part(b + 1, 1)

            split_w(0)
            split_w(1)
            split_x(0)
            split_w(2)
            split_w(3)
            gate(0, 0)
            high_part(0, 0)
            gate(0, 1)
            batch(0, first=True, more=True)
            for b in range(1, B - 1):
                batch(b, more=(b < B - 2))
            batch(B - 1, last=True)
            act.preload_act_table(ACT.Exp)
            normalise_x1(B - 1)
            act.wait_ge(s_shifted, B)
            act.activation(expo[:, :], shift_ps[:, 0:1], ACT.Exp).then_inc(s_exp, 1)
            act.preload_act_table(ACT.Gelu)
            for pair in range(NF // 2):
                tiles = slice(2 * pair, 2 * pair + 2)
                act.wait_ge(s_hid, pair + 1)
                act.activation(gT[:, tiles, :], hid_ps[pair], ACT.Gelu).then_inc(s_g, 1)
                act.wait_ge(s_g, pair + 1)
                act.activation(gT_hi[:, tiles, :], gT[:, tiles, :], ACT.Copy).then_inc(s_gThi, 1)

        @block.gpsimd
        def _(pool):
            pool.iota(col_minus_row[:, :], [[1, S]], base=0, channel_multiplier=-1).then_inc(s_iota, 1)
            pool.memset(minus_half[:, :], -0.5).then_inc(s_half, 1)
            pool.iota(rank_iota[:, :], [[1, TOP]], base=0, channel_multiplier=0).then_inc(s_iota, 1)
            pool.iota(token_row[:, :], [[P, NT]], base=0, channel_multiplier=1).then_inc(s_trow, 1)
            pool.memset(select[:, :, :], 0.0).then_inc(s_zero, 1)

            def inverse_root(variance, shifted_var, target, shifted_signal, signal, count):
                pool.tensor_scalar(shifted_var, variance, EPS, None, ALU.add).then_inc(shifted_signal, 1)
                pool.wait_ge(shifted_signal, count)
                pool.tensor_tensor(target, shifted_var, minus_half[:, 0:target.shape[1]], ALU.pow).then_inc(signal, 1)

            def rstd_x(b):
                tiles = slice(NJ * b, NJ * b + NJ)
                pool.wait_ge(s_mean, b + 1)
                inverse_root(mean_var[:, tiles, 1], var_eps[:, tiles], rstd[:, tiles], s_veps, s_rstd, b + 1)

            def rstd_x1(b):
                pool.wait_ge(s_mean2, b + 1)
                wait(pool, s_xn2, b)
                inverse_root(mean_var2[:, :, 1], var_eps2[:, :], rstd2[:, :], s_veps2, s_rstd2, b + 1)

            def split_w(e):
                pool.wait_ge(s_whi, e + 1)
                pool.tensor_tensor(w_lo[:, e], wT_in[:, e], w_hi[:, e].bitcast(F32), ALU.subtract).then_inc(s_wlo[e], 1)

            def low_part(b, e):
                u = E * b + e
                pool.wait_ge(s_ghi, u + 1)
                pool.tensor_tensor(gu_lo[:, e], gu[:, e], gu_hi[:, e].bitcast(F32),
                                   ALU.subtract).then_inc(s_glo, 1)

            def add_base(b):
                pool.wait_ge(s_xn2, b + 1)
                pool.tensor_tensor(base[:, NJ * b:NJ * b + NJ, :], x1[:, NJ * b:NJ * b + NJ, :],
                                   xn2[:, NJ * b:NJ * b + NJ, :],
                                   ALU.add).then_inc(s_base, 1)

            def split_w2(part):
                pool.wait_ge(s_w2hi, part + 1)
                tiles = slice(NF // W2_PARTS * part, NF // W2_PARTS * (part + 1))
                pool.tensor_tensor(w2_lo[:, tiles], w2_in[:, tiles], w2_hi[:, tiles].bitcast(F32),
                                   ALU.subtract).then_inc(s_w2lo, 1)

            def choose(b):
                pool.wait_ge(s_count, 2 * NJ * (b + 1))
                pool.wait_ge(s_ranks, 1)
                pool.wait_ge(s_zero, 1)
                for j in range(NJ):
                    t = NJ * b + j
                    s = pool.tensor_scalar(select[:, t, TOP * b:TOP * b + TOP], rank_of_slot[:, :], above[:, t:t + 1],
                                           tied[:, t:t + 1], ALU.subtract, ALU.is_equal)
                s.then_inc(s_select, 1)

            def shift(b):
                pool.wait_ge(s_top, b + 1)
                pool.tensor_scalar(shift_row[:, NJ * b:NJ * b + NJ, 0], logits[:, NJ * b:NJ * b + NJ],
                                   top_logit[:, b:b + 1], None, ALU.subtract).then_inc(s_shift, 1)

            def batch(b, first=False, last=False):
                if not first:
                    rstd_x1(b - 1)
                low_part(b, 2)
                if b > 1:
                    choose(b - 2)
                    shift(b - 2)
                if not (first or last):
                    split_w2(b)
                low_part(b, 3)
                if first:
                    rstd_x(3)
                    split_w2(b)
                if not first:
                    add_base(b - 1)
                if not last:
                    low_part(b + 1, 0)
                    low_part(b + 1, 1)

            pool.wait_ge(s_half, 1)
            rstd_x(0)
            split_w(0)
            split_w(2)
            rstd_x(1)
            low_part(0, 0)
            rstd_x(2)
            low_part(0, 1)
            batch(0, first=True)
            for b in range(1, B - 1):
                batch(b)
            batch(B - 1, last=True)
            shift(B - 2)
            rstd_x1(B - 1)
            choose(B - 2)
            add_base(B - 1)
            split_w2(B - 1)
            out_rows = out.rearrange("b s d -> (b s) d")
            pool.wait_ge(s_index, 1)
            pool.wait_ge(d_out, 16 * B)
            pool.indirect_dma_start(base_slots[:, :], None, out_rows,
                                    bass.IndirectOffsetOnAxis(row_index[:, 0:1], 0)).then_inc(d_base, 16)
            pool.wait_ge(s_rows, 1)
            pool.indirect_dma_start(out_rows, bass.IndirectOffsetOnAxis(row_index[:, 0:1], 0),
                                    slot_rows[:, :], None).then_inc(d_scatter, 16)
            pool.wait_ge(d_scatter, 16)

        @block.vector
        def _(dve):
            def statistics(source, st, mv, tiles, signal_st, count, signal):
                for j, t in enumerate(tiles):
                    dve.bn_stats(st[:, j, :], source[:, t, :]).then_inc(signal_st, 1)
                dve.wait_ge(signal_st, count)
                for j, t in enumerate(tiles):
                    aggr = dve.bn_aggr(mv[:, j, :], st[:, j, :])
                aggr.then_inc(signal, 1)

            def stats_x1(b):
                wait(dve, s_mean2, b)
                wait(dve, s_xn2, b)
                wait(dve, s_veps2, b)
                dve.wait_ge(s_x1, NJ * E * (b + 1))
                statistics(x1, stats2, mean_var2, [NJ * b + j for j in range(NJ)], s_stats2, NJ * b + NJ, s_mean2)

            def normalise_x(b):
                dve.wait_ge(s_rstd, b + 1)
                for j in range(NJ):
                    t = NJ * b + j
                    n = dve.tensor_scalar(xn[:, j, :], x_in[:, t, :], mean_var[:, t, 0:1], rstd[:, t:t + 1],
                                          ALU.subtract, ALU.mult)
                n.then_inc(s_xn, 1)

            def router_dot(b):
                dve.wait_ge(s_mean2, b + 1)
                wait(dve, s_logit, NJ * b)
                for j in range(NJ):
                    t = NJ * b + j
                    dve.scalar_tensor_tensor(out=product[:, j, :], in0=x1[:, t, :], scalar=mean_var2[:, j, 0:1],
                                             in1=wr_all[:, :], op0=ALU.subtract, op1=ALU.mult,
                                             accum_out=dots[:, j:j + 1]).then_inc(s_dot, 1)

            def router(b):
                dve.wait_ge(s_rstd2, b + 1)
                dve.wait_ge(s_dot, NJ * b + NJ)
                for j in range(NJ):
                    t = NJ * b + j
                    dve.scalar_tensor_tensor(out=logits[:, t:t + 1], in0=dots[:, j:j + 1], scalar=rstd2[:, j:j + 1],
                                             in1=br_all[:, :], op0=ALU.mult, op1=ALU.add).then_inc(s_logit, 1)
                dve.scalar_tensor_tensor(out=minus_mean2[:, :], in0=mean_var2[:, :, 0], scalar=-1.0,
                                         in1=rstd2[:, :], op0=ALU.mult, op1=ALU.mult).then_inc(s_mmean2, 1)

            def split_x(b):
                dve.wait_ge(s_xhi, b + 1)
                dve.tensor_tensor(xT_lo[:, b], xT_ps[:, :, :], xT_hi[:, b].bitcast(F32), ALU.subtract).then_inc(s_xlo, 1)

            def gate(b, e):
                u = E * b + e
                dve.wait_ge(s_silu, u + 1)
                wait(dve, s_glo, u - E + 1)
                dve.tensor_tensor(gu[:, e], silu[:, e % 2], h_bank(b, e)[:, :, :], ALU.mult).then_inc(s_gu, 1)

            def add_tile(b, e, j, source):
                t = NJ * b + j
                if e > 0:
                    dve.wait_ge(s_x1, NJ * (E * b + e - 1) + j + 1)
                dve.scalar_tensor_tensor(out=x1[:, t, :], in0=source, scalar=mask[:, e, t:t + 1],
                                         in1=(x_in if e == 0 else x1)[:, t, :], op0=ALU.mult,
                                         op1=ALU.add).then_inc(s_x1, 1)

            def accumulate(b, e):
                dve.wait_ge(s_y, E * b + e + 1)
                for j in range(NJ):
                    add_tile(b, e, j, y_ps[e % 2][:, j, :])

            def finish_last():
                b, u = B - 1, B * E - 1
                dve.wait_ge(s_mean2, b)
                dve.wait_ge(s_xn2, b)
                for j in range(NJ):
                    dve.wait_ge(s_y, u + 1 + j)
                    add_tile(b, E - 1, j, (h_ps[0] if j > 0 else y_ps[1])[:, j, :])
                    dve.wait_ge(s_x1, NJ * u + j + 1)
                    dve.bn_stats(stats2[:, j, :], x1[:, NJ * b + j, :]).then_inc(s_stats2, 1)
                dve.wait_ge(s_stats2, NJ * B)
                for j in range(NJ):
                    aggr = dve.bn_aggr(mean_var2[:, j, :], stats2[:, j, :])
                aggr.then_inc(s_mean2, 1)

            def count(b, tiles=range(NJ)):
                dve.wait_ge(s_lrow, b + 1)
                wait(dve, s_count, 2 * NJ * b)
                row = row_ps(b)
                for j in tiles:
                    t = NJ * b + j
                    n = P * (j + 1)
                    dve.tensor_scalar(scratch_above[:, j, :], row, logits[:, t:t + 1], 0.0, ALU.is_gt,
                                      ALU.add, accum_out=above[:, t:t + 1]).then_inc(s_count, 1)
                    dve.scalar_tensor_tensor(out=scratch_tied[:, j, 0:n], in0=row[:, 0:n],
                                             scalar=logits[:, t:t + 1], in1=earlier[:, j, 0:n], op0=ALU.is_equal,
                                             op1=ALU.mult, accum_out=tied[:, t:t + 1]).then_inc(s_count, 1)

            def find_top(b):
                dve.reduce_max(top_logit[:, b:b + 1], row_ps(b), AX_X).then_inc(s_top, 1)

            def choose_last():
                b = B - 1
                dve.wait_ge(s_zero, 1)
                dve.wait_ge(s_ranks, 1)
                dve.wait_ge(s_count, 2 * NJ * (b + 1))
                for j in range(NJ):
                    t = NJ * b + j
                    s = dve.tensor_scalar(select[:, t, TOP * b:TOP * b + TOP], rank_of_slot[:, :], above[:, t:t + 1],
                                          tied[:, t:t + 1], ALU.subtract, ALU.is_equal)
                s.then_inc(s_select_last, 1)
                find_top(b)
                dve.wait_ge(s_top, b + 1)
                dve.tensor_scalar(shift_row[:, NJ * b:NJ * b + NJ, 0], logits[:, NJ * b:NJ * b + NJ],
                                  top_logit[:, b:b + 1], None, ALU.subtract).then_inc(s_shift_last, 1)

            def split_w(e):
                dve.wait_ge(s_whi, e + 1)
                dve.tensor_tensor(w_lo[:, e], wT_in[:, e], w_hi[:, e].bitcast(F32), ALU.subtract).then_inc(s_wlo[e], 1)

            def stats_x(b):
                dve.wait_ge(d_x[b], 16)
                tiles = slice(NJ * b, NJ * b + NJ)
                statistics(x_in, stats[:, tiles, :], mean_var[:, tiles, :], range(NT)[tiles], s_stats, NJ * b + NJ,
                           s_mean)

            def scale_mean(b):
                tiles = slice(NJ * b, NJ * b + NJ)
                dve.wait_ge(s_rstd, b + 1)
                dve.scalar_tensor_tensor(out=minus_mean[:, tiles], in0=mean_var[:, tiles, 0], scalar=-1.0,
                                         in1=rstd[:, tiles], op0=ALU.mult, op1=ALU.mult).then_inc(s_mmean, 1)

            def batch(b, first=False, last=False):
                if not first:
                    stats_x1(b - 1)
                gate(b, 2)
                if first:
                    scale_mean(2)
                else:
                    router_dot(b - 1)
                    router(b - 1)
                if first or last:
                    gate(b, 3)
                if first:
                    split_x(b + 1)
                accumulate(b, 0)
                if first:
                    stats_x(3)
                elif not last:
                    split_x(b + 1)
                    gate(b, 3)
                if last:
                    count(b - 1, [0])
                accumulate(b, 1)
                if first:
                    scale_mean(3)
                elif not last:
                    count(b - 1)
                if not first:
                    find_top(b - 1)
                if not last:
                    gate(b + 1, 0)
                accumulate(b, 2)
                if not last:
                    gate(b + 1, 1)
                    accumulate(b, 3)

            dve.memset(warm[:, :], 0.0).then_inc(s_warm, 1)
            dve.memset(ones[:, :], 1.0).then_inc(s_const, 1)
            dve.memset(same_batch[:, :], 0.0).then_inc(s_same0, 1)
            dve.memset(at_least[:, 0, :], 1.0).then_inc(s_geq, 1)
            dve.memset(at_least[:, E, :], 0.0).then_inc(s_geq, 1)
            dve.wait_ge(s_same0, 1)
            for b in range(B):
                m = dve.memset(same_batch[TOP * b:TOP * b + TOP, TOP * b:TOP * b + TOP], 1.0)
            m.then_inc(s_same, 1)
            dve.wait_ge(s_iota, 1)
            dve.tensor_scalar(ident[:, :], col_minus_row[:, 0:P], 0.0, None, ALU.is_equal).then_inc(s_const, 1)
            dve.tensor_scalar(earlier[:, 0, :], col_minus_row[:, :], 0.0, None, ALU.is_lt).then_inc(s_const, 1)
            dve.tensor_scalar(earlier[:, 1, :], col_minus_row[:, :], float(P), None, ALU.is_lt).then_inc(s_const, 1)
            dve.wait_ge(s_iota, 2)
            dve.tensor_copy(rank_of_slot[:, :], rank_iota[:, :]).then_inc(s_ranks, 1)
            stats_x(0)
            normalise_x(0)
            dve.wait_ge(d_tok, 16)
            for e in range(1, E):
                dve.tensor_scalar(at_least[:, e, :], tok[:, :], float(e * PER_EXPERT), None,
                                  ALU.is_ge).then_inc(s_geq, 1)
            dve.wait_ge(s_geq, E + 1)
            dve.tensor_tensor(mask[:, :, :], at_least[:, 0:E, :], at_least[:, 1:E + 1, :],
                              ALU.subtract).then_inc(s_mask, 1)
            split_w(1)
            split_x(0)
            stats_x(1)
            split_w(3)
            gate(0, 0)
            scale_mean(1)
            stats_x(2)
            gate(0, 1)
            dve.wait_ge(s_mask, 1)
            batch(0, first=True)
            dve.wait_ge(s_trow, 1)
            dve.tensor_copy(shift_row[:, :, 1], token_row[:, :])
            dve.wait_ge(d_wr, 32)
            dve.wait_ge(s_const, 4)
            for b in range(1, B - 1):
                batch(b)
            batch(B - 1, last=True)
            finish_last()
            router_dot(B - 1)
            router(B - 1)
            count(B - 2, [1])
            count(B - 1)
            choose_last()
            dve.wait_ge(s_gather, B)
            dve.tensor_copy(fxT[:, :, :], fxT_ps).then_inc(s_fx, 1)
            dve.wait_ge(s_exp, 1)
            dve.tensor_copy(row_index[:, :], shift_ps[:, 1:2]).then_inc(s_index, 1)

            def gelu_low(pair):
                tiles = slice(2 * pair, 2 * pair + 2)
                dve.wait_ge(s_gThi, pair + 1)
                dve.tensor_tensor(gT_lo[:, tiles, :], gT[:, tiles, :], gT_hi[:, tiles, :].bitcast(F32),
                                  ALU.subtract).then_inc(s_gTlo, 1)

            for pair in range(NF // 2):
                gelu_low(pair)
            dve.wait_ge(s_sum, 1)
            dve.reciprocal(expo_inv[:, :], sum_ps).then_inc(s_einv, 1)
            dve.wait_ge(s_einv, 1)
            dve.tensor_tensor(weight[:, :], expo[:, :], expo_inv[:, :], ALU.mult).then_inc(s_weight, 1)
            dve.wait_ge(s_weight, 1)
            dve.wait_ge(d_b, 32)
            dve.wait_ge(d_base, 16)
            dve.scalar_tensor_tensor(out=base_slots[:, :], in0=b2_all[:, :], scalar=weight[:, 0:1],
                                     in1=base_slots[:, :], op0=ALU.mult, op1=ALU.add).then_inc(s_bias, 1)
            dve.wait_ge(s_bias, 1)
            dve.wait_ge(s_ffn, 1)
            dve.scalar_tensor_tensor(out=slot_rows[:, :], in0=ffn_ps, scalar=weight[:, 0:1], in1=base_slots[:, :],
                                     op0=ALU.mult, op1=ALU.add).then_inc(s_rows, 1)


def kernel(x, itok_BxS_13_99985, ctx_2048, L0_ffn_Wr, L0_ffn_br, L0_ffn_W1, L0_ffn_b1, L0_ffn_W2, L0_ffn_b2):
    import numpy as np
    import concourse.bacc as bacc
    from concourse.bass_utils import run_bass_kernel_spmd

    B, S, D = x.shape
    flat = np.ascontiguousarray
    arrays = {
        "x": flat(x),
        "tokens": flat(np.asarray(itok_BxS_13_99985).reshape(-1, P).T),
        "wT": flat(np.asarray(ctx_2048).transpose(0, 2, 1)),
        "wr": flat(np.asarray(L0_ffn_Wr).reshape(D)),
        "br": flat(L0_ffn_br),
        "w1": flat(L0_ffn_W1),
        "b1": flat(np.asarray(L0_ffn_b1).reshape(1, -1)),
        "w2": flat(L0_ffn_W2),
        "b2": flat(L0_ffn_b2),
    }
    nc = bacc.Bacc("TRN2", target_bir_lowering=False, num_devices=1)
    args = [nc.dram_tensor(f"in_{n}", a.shape, mybir.dt.from_np(a.dtype), kind="ExternalInput").ap()
            for n, a in arrays.items()]
    args.append(nc.dram_tensor("out", (B, S, D), F32, kind="ExternalOutput").ap())
    fused_layers(nc, *args)
    r = run_bass_kernel_spmd(nc, [{f"in_{n}": a for n, a in arrays.items()}], core_ids=[0])
    return r.results[0]["out"]
```
